# Optimizing a Trainium2 kernel written in Bass

```python
import numpy as np
import jax
import jax.numpy as jnp

def _softmax(x, axis=-1):
    return jax.nn.softmax(x, axis=axis)
def _gelu(x):
    return jax.nn.gelu(x, approximate=True)
def _silu(x):
    return jax.nn.silu(x)
def _sigmoid(x):
    return jax.nn.sigmoid(x)
def _layernorm(x, axis=-1, eps=1e-5):
    m = jnp.mean(x, axis=axis, keepdims=True)
    v = jnp.var(x, axis=axis, keepdims=True)
    return (x - m) / jnp.sqrt(v + eps)
def _scatter_add(tgt, idx, src, axis=0):
    return tgt.at[idx].add(src)
def _segment_sum(src, seg, n):
    return jax.ops.segment_sum(src, seg, n)

kernel_name = 'mk_metaformer_d1_conv_nchw128_570e5f'

def setup_inputs(seed: int = 0):
    np.random.seed(seed)
    _w = jnp.asarray
    def _rec_inputs():
        import jax
        import jax.numpy as jnp
        _gk = jax.random.key(seed)
        x = -3.91e-05 + 0.9999 * jax.random.normal(jax.random.fold_in(_gk, 1), (32, 128, 110, 110), jnp.float32)
        return x
    x = _rec_inputs()
    def _L0_conv_setup():
        import jax, jax.numpy as jnp
        import numpy as np
        C = 128
        H = 110
        K = 768
        NH = 8
        EPS_BN = 1e-05
        EPS_LN = 1e-05

        def make_pos(seq_len, dim):
            pos = np.arange(seq_len, dtype=np.float32)[:, None]
            div = np.exp(np.arange(0, dim, 2, dtype=np.float32) * -(np.log(10000.0) / dim))
            pe = np.zeros((seq_len, dim), dtype=np.float32)
            pe[:, 0::2] = np.sin(pos * div)
            pe[:, 1::2] = np.cos(pos * div)
            return jnp.asarray(pe)

        def _layernorm(t, g, b):
            mu = t.mean(-1, keepdims=True)
            var = t.var(-1, keepdims=True)
            return (t - mu) / jnp.sqrt(var + EPS_LN) * g + b
        key = jax.random.key(seed)
        ks = jax.random.split(key, 10)
        B = 32
        s = 0.05
        return {'x': jax.random.normal(ks[0], (B, C, H, H), jnp.float32), 'conv_w': jax.random.normal(ks[1], (1, C, 7, 7), jnp.float32) * s, 'conv_b': jnp.zeros((1,), jnp.float32), 'bn_g': jnp.ones((1,), jnp.float32), 'bn_b': jnp.zeros((1,), jnp.float32), 'bn_m': jnp.zeros((1,), jnp.float32), 'bn_v': jnp.ones((1,), jnp.float32), 'w_qkv': jax.random.normal(ks[2], (3 * C, C), jnp.float32) * s, 'b_qkv': jnp.zeros((3 * C,), jnp.float32), 'w_o': jax.random.normal(ks[3], (C, C), jnp.float32) * s, 'b_o': jnp.zeros((C,), jnp.float32), 'ln1_g': jnp.ones((C,), jnp.float32), 'ln1_b': jnp.zeros((C,), jnp.float32), 'w1': jax.random.normal(ks[4], (2 * C, C), jnp.float32) * s, 'b1': jnp.zeros((2 * C,), jnp.float32), 'w2': jax.random.normal(ks[5], (C, 2 * C), jnp.float32) * s, 'b2': jnp.zeros((C,), jnp.float32), 'ln2_g': jnp.ones((C,), jnp.float32), 'ln2_b': jnp.zeros((C,), jnp.float32)}
    _L0_conv_all = _L0_conv_setup()
    _L0_conv_in = {k: v for k, v in _L0_conv_all.items() if k in ('conv_w', 'conv_b', 'bn_g', 'bn_b', 'bn_m', 'bn_v', 'w_qkv', 'b_qkv', 'w_o', 'b_o', 'ln1_g', 'ln1_b', 'w1', 'b1', 'w2', 'b2', 'ln2_g', 'ln2_b', )}
    del _L0_conv_all

    def _L0_ffn_setup():
        import jax, jax.numpy as jnp
        import numpy as np
        B, S, D, E, H, O, K = (512, 2048, 128, 64, 512, 128, 8)
        key = jax.random.key(seed)
        k0, k1, k2, k3 = jax.random.split(key, 4)
        x = jax.random.normal(k0, (B, S, D), dtype=jnp.float32)
        gate_w = jax.random.normal(k1, (E, D), dtype=jnp.float32) * (1.0 / np.sqrt(D))
        gate_b = jnp.zeros((E,), dtype=jnp.float32)
        weight1 = jax.random.uniform(k2, (E, D + 1, H), dtype=jnp.float32, minval=-1.0, maxval=1.0) * (1.0 / np.sqrt(D + 1))
        weight2 = jax.random.uniform(k3, (E, H + 1, O), dtype=jnp.float32, minval=-1.0, maxval=1.0) * (1.0 / np.sqrt(H + 1))
        return {'x': x, 'gate_w': gate_w, 'gate_b': gate_b, 'weight1': weight1, 'weight2': weight2}
    _L0_ffn_all = _L0_ffn_setup()
    _L0_ffn_in = {k: v for k, v in _L0_ffn_all.items() if k in ('gate_w', 'gate_b', 'weight1', 'weight2', )}
    del _L0_ffn_all

    return {
        "x": x,
        "L0_conv_conv_w": _L0_conv_in["conv_w"],
        "L0_conv_conv_b": _L0_conv_in["conv_b"],
        "L0_conv_bn_g": _L0_conv_in["bn_g"],
        "L0_conv_bn_b": _L0_conv_in["bn_b"],
        "L0_conv_bn_m": _L0_conv_in["bn_m"],
        "L0_conv_bn_v": _L0_conv_in["bn_v"],
        "L0_conv_w_qkv": _L0_conv_in["w_qkv"],
        "L0_conv_b_qkv": _L0_conv_in["b_qkv"],
        "L0_conv_w_o": _L0_conv_in["w_o"],
        "L0_conv_b_o": _L0_conv_in["b_o"],
        "L0_conv_ln1_g": _L0_conv_in["ln1_g"],
        "L0_conv_ln1_b": _L0_conv_in["ln1_b"],
        "L0_conv_w1": _L0_conv_in["w1"],
        "L0_conv_b1": _L0_conv_in["b1"],
        "L0_conv_w2": _L0_conv_in["w2"],
        "L0_conv_b2": _L0_conv_in["b2"],
        "L0_conv_ln2_g": _L0_conv_in["ln2_g"],
        "L0_conv_ln2_b": _L0_conv_in["ln2_b"],
        "L0_ffn_gate_w": _L0_ffn_in["gate_w"],
        "L0_ffn_gate_b": _L0_ffn_in["gate_b"],
        "L0_ffn_weight1": _L0_ffn_in["weight1"],
        "L0_ffn_weight2": _L0_ffn_in["weight2"],
    }

def reference(x, L0_conv_conv_w, L0_conv_conv_b, L0_conv_bn_g, L0_conv_bn_b, L0_conv_bn_m, L0_conv_bn_v, L0_conv_w_qkv, L0_conv_b_qkv, L0_conv_w_o, L0_conv_b_o, L0_conv_ln1_g, L0_conv_ln1_b, L0_conv_w1, L0_conv_b1, L0_conv_w2, L0_conv_b2, L0_conv_ln2_g, L0_conv_ln2_b, L0_ffn_gate_w, L0_ffn_gate_b, L0_ffn_weight1, L0_ffn_weight2):
    import jax
    import jax.numpy as jnp
    def _L0_conv_ref(x, conv_w, conv_b, bn_g, bn_b, bn_m, bn_v, w_qkv, b_qkv, w_o, b_o, ln1_g, ln1_b, w1, b1, w2, b2, ln2_g, ln2_b):
        import jax, jax.numpy as jnp
        import numpy as np
        C = 128
        H = 110
        K = 768
        NH = 8
        EPS_BN = 1e-05
        EPS_LN = 1e-05

        def make_pos(seq_len, dim):
            pos = np.arange(seq_len, dtype=np.float32)[:, None]
            div = np.exp(np.arange(0, dim, 2, dtype=np.float32) * -(np.log(10000.0) / dim))
            pe = np.zeros((seq_len, dim), dtype=np.float32)
            pe[:, 0::2] = np.sin(pos * div)
            pe[:, 1::2] = np.cos(pos * div)
            return jnp.asarray(pe)

        def _layernorm(t, g, b):
            mu = t.mean(-1, keepdims=True)
            var = t.var(-1, keepdims=True)
            return (t - mu) / jnp.sqrt(var + EPS_LN) * g + b
        B = x.shape[0]
        y = jax.lax.conv_general_dilated(x, conv_w, window_strides=(1, 1), padding=[(15, 15), (15, 15)], rhs_dilation=(5, 5), dimension_numbers=('NCHW', 'OIHW', 'NCHW'))
        y = y + conv_b[None, :, None, None]
        scale = (bn_g / jnp.sqrt(bn_v + EPS_BN))[None, :, None, None]
        y = (y - bn_m[None, :, None, None]) * scale + bn_b[None, :, None, None]
        imp = jax.nn.sigmoid(jax.nn.gelu(y, approximate=False))
        xs = x * imp
        flat = imp[:, 0].reshape(B, -1)
        _, idx = jax.lax.top_k(flat, K)
        idx = jnp.sort(idx, axis=1)
        xf = xs.reshape(B, C, H * H).transpose(0, 2, 1)
        tokens = jnp.take_along_axis(xf, idx[:, :, None], axis=1)
        tokens = tokens + make_pos(H * H, C)[idx]
        qkv = tokens @ w_qkv.T + b_qkv
        q, k_, v = jnp.split(qkv, 3, axis=-1)
        hd = C // NH

        def heads(t):
            return t.reshape(B, K, NH, hd).transpose(0, 2, 1, 3)
        q, k_, v = (heads(q), heads(k_), heads(v))
        scores = jnp.einsum('bhqd,bhkd->bhqk', q, k_) * (1.0 / np.sqrt(hd)).astype(x.dtype)
        attn = jax.nn.softmax(scores, axis=-1)
        o = jnp.einsum('bhqk,bhkd->bhqd', attn, v).transpose(0, 2, 1, 3).reshape(B, K, C)
        o = o @ w_o.T + b_o
        t1 = _layernorm(tokens + o, ln1_g, ln1_b)
        ff = jax.nn.relu(t1 @ w1.T + b1) @ w2.T + b2
        t2 = _layernorm(t1 + ff, ln2_g, ln2_b)
        xf = xf.at[jnp.arange(B)[:, None], idx].set(t2)
        return xf.transpose(0, 2, 1).reshape(B, C, H, H)

    def _L0_ffn_ref(x, gate_w, gate_b, weight1, weight2):
        import jax, jax.numpy as jnp
        import numpy as np
        B, S, D, E, H, O, K = (512, 2048, 128, 64, 512, 128, 8)
        Bn, Sn, Dn = x.shape
        logits = jnp.einsum('bsd,ed->bse', x, gate_w) + gate_b
        probs = jax.nn.softmax(logits, axis=1)
        vals, idx = jax.lax.top_k(probs.transpose(0, 2, 1), K)
        topv = vals.transpose(0, 2, 1)
        topi = idx.transpose(0, 2, 1)
        flat_idx = topi.reshape(Bn, K * E)
        gathered = jnp.take_along_axis(x, flat_idx[:, :, None], axis=1)
        gathered = gathered.reshape(Bn, K, E, Dn)
        pooled = jnp.einsum('bked,bke->bed', gathered, topv)
        ones = jnp.ones((E, Bn, 1), dtype=x.dtype)
        h = jnp.concatenate([pooled.transpose(1, 0, 2), ones], axis=-1)
        h = jax.nn.gelu(jnp.einsum('ebd,edh->ebh', h, weight1), approximate=False)
        h = jnp.concatenate([h, ones], axis=-1)
        out = jnp.einsum('ebh,eho->ebo', h, weight2)
        out = out.transpose(1, 0, 2)
        weighted = jnp.einsum('beo,bke->bkeo', out, topv).reshape(Bn, K * E, O)
        outputs = jnp.zeros((Bn, Sn, O), dtype=x.dtype)
        outputs = outputs.at[jnp.arange(Bn)[:, None], flat_idx].add(weighted)
        return outputs

    def _gn(v, G=32, eps=1e-5):
        B_, C_, H_, W_ = v.shape
        g = v.reshape(B_, G, C_ // G, H_, W_)
        m = jnp.mean(g, axis=(2, 3, 4), keepdims=True)
        s = jnp.var(g, axis=(2, 3, 4), keepdims=True)
        return ((g - m) / jnp.sqrt(s + eps)).reshape(v.shape)

    def _ln_c(v, eps=1e-6):
        m = jnp.mean(v, axis=1, keepdims=True)
        s = jnp.var(v, axis=1, keepdims=True)
        return (v - m) / jnp.sqrt(s + eps)

    def _ln_t(v, eps=1e-5):
        m = jnp.mean(v, axis=-1, keepdims=True)
        s = jnp.var(v, axis=-1, keepdims=True)
        return (v - m) / jnp.sqrt(s + eps)

    def _to_tokens(v):
        B_, C_, H_, W_ = v.shape
        return v.reshape(B_, C_, H_ * W_).transpose(0, 2, 1)
    def _from_tokens(t, like):
        B_, C_, H_, W_ = like.shape
        return t.transpose(0, 2, 1).reshape(B_, C_, H_, W_)

    x = x + _L0_conv_ref(_ln_c(x), L0_conv_conv_w, L0_conv_conv_b, L0_conv_bn_g, L0_conv_bn_b, L0_conv_bn_m, L0_conv_bn_v, L0_conv_w_qkv, L0_conv_b_qkv, L0_conv_w_o, L0_conv_b_o, L0_conv_ln1_g, L0_conv_ln1_b, L0_conv_w1, L0_conv_b1, L0_conv_w2, L0_conv_b2, L0_conv_ln2_g, L0_conv_ln2_b)
    t = _to_tokens(x)
    t = t + _L0_ffn_ref(_ln_t(t), L0_ffn_gate_w, L0_ffn_gate_b, L0_ffn_weight1, L0_ffn_weight2)
    x = _from_tokens(t, x)
    return x


_drawn_inputs = setup_inputs


def setup_inputs(seed=0):
    import zlib

    import numpy as np

    out = dict(_drawn_inputs(seed))
    spreads = {'L0_conv_b_qkv': (0.0, 0.8),
     'L0_conv_b_o': (0.0, 2.0),
     'L0_conv_ln1_g': (1.0, 0.2),
     'L0_conv_ln1_b': (0.0, 0.548),
     'L0_conv_b1': (0.0, 0.8),
     'L0_conv_b2': (0.0, 0.512),
     'L0_conv_ln2_g': (1.0, 0.2),
     'L0_conv_ln2_b': (0.0, 0.567),
     'L0_ffn_gate_b': (0.0, 0.8)}
    factors = {'L0_conv_w_qkv': 5.607,
     'L0_conv_w_o': 4.916,
     'L0_ffn_gate_w': 8.0,
     'L0_ffn_weight1': 8.0,
     'L0_ffn_weight2': 8.0}
    for name, (base, spread) in spreads.items():
        noise = np.random.default_rng([zlib.crc32(name.encode()), seed]).standard_normal(out[name].shape)
        drawn = base * np.exp(spread * noise) if base else spread * noise
        out[name] = jnp.asarray(drawn.astype(out[name].dtype))
    for name, factor in factors.items():
        out[name] = (out[name] * factor).astype(out[name].dtype)
    return out
```

```python
import numpy as np
import concourse.bass as bass
from concourse import mybir
from contextlib import ExitStack

F32 = mybir.dt.float32
BF16 = mybir.dt.bfloat16
U32 = mybir.dt.uint32
ALU = mybir.AluOpType
ACT = mybir.ActivationFunctionType
AX = mybir.AxisListType

C = 128
H = 110
NPIX = H * H
NLOADS = 24
TAPS, DIL, PAD = 7, 5, 15
NTAP = TAPS * TAPS
KTOK = 768
NCH = KTOK // 128
HALF = KTOK // 2
NH, HD = 8, 16
SLOTS = 6
KROWS = SLOTS * HD
E = 64
TOPE = 8
HID = 512
MAPS = NTAP + E
ROWS = NPIX + KTOK
NEG = -1.0e30
FAR = 3.0e7
CHUNK_ROWS = (12,) * 8 + (8, 6)
GROUPS = -(-H // 4)
LAST_GROUP = [-(-sum(CHUNK_ROWS[:t + 1]) // 4) for t in range(10)]
SEARCH = 9
AR = 22
LG = 28
DVE_PER, ACT_PER = 700, 200

C_ID, C_ONE, C_LT, C_SH = 0, 128, 256, 384
C_IOTA = C_SH + TAPS * H
C_HROW = C_IOTA + 128
C_W = C_HROW + H
C_TH = C_W + 1
C_S1 = C_TH + 8
C_RAMP = C_S1 + 1
NCONST = C_RAMP + 7


def constants():
    c = np.zeros((128, NCONST), np.float32)
    p = np.arange(128)
    c[:, C_ID:C_ID + 128] = np.eye(128)
    c[:, C_ONE:C_ONE + 128] = 1
    c[:, C_LT:C_LT + 128] = p[:, None] < p[None]
    for j in range(TAPS):
        c[:, C_SH + j * H:C_SH + (j + 1) * H] = p[:, None] == p[None, :H] + DIL * j - PAD
    c[:, C_IOTA:C_IOTA + 128] = p[None]
    c[:, C_HROW:C_HROW + H] = p[None, :H]
    c[:, C_W] = p
    c[:, C_TH:C_TH + 7] = np.arange(1, 8)[None]
    c[:, C_S1] = (p >= E) * ROWS
    c[:, C_RAMP:C_RAMP + 7] = 128 * np.arange(7)[None]
    return c


def positions():
    pos = np.arange(NPIX, dtype=np.float32)[:, None]
    div = np.exp(np.arange(0, C, 2, dtype=np.float32) * -(np.log(10000.0) / C))
    pe = np.zeros((NPIX, C), dtype=np.float32)
    pe[:, 0::2] = np.sin(pos * div)
    pe[:, 1::2] = np.cos(pos * div)
    return pe


class Own:

    def __init__(self, eng, sem, k, per):
        self.eng, self.sem, self.k, self.per, self.n = eng, sem, k, per, 0

    def step(self, ins):
        ins.then_inc(self.sem, 1)
        self.n += 1

    def wait(self):
        self.eng.wait_ge(self.sem, self.k * self.per + self.n)

    def link(self, ins):
        self.step(ins)
        self.wait()

    def pad(self):
        assert self.n < self.per, self.n
        self.eng.sem_inc(self.sem, self.per - self.n)



def bc(ap, shape, at):
    return ap.unsqueeze(at).broadcast_to(shape)


def combine(v, own, mv, bs, bh):
    own.step(v.tensor_tensor(mv[:, :, 0], bs[:, :, 1], bs[:, :, 4], ALU.add))
    own.step(v.tensor_tensor(bh[:, :], bs[:, :, 1], bs[:, :, 4], ALU.subtract))
    own.link(v.tensor_tensor(mv[:, :, 1], bs[:, :, 2], bs[:, :, 5], ALU.add))
    own.step(v.tensor_scalar(mv[:, :, 0], mv[:, :, 0], 0.5, None, ALU.mult))
    own.step(v.tensor_scalar(mv[:, :, 1], mv[:, :, 1], 1.0 / C, None, ALU.mult))
    own.link(v.tensor_scalar(bh[:, :], bh[:, :], 0.5, None, ALU.mult))
    own.link(v.tensor_tensor(bh[:, :], bh[:, :], bh[:, :], ALU.mult))
    own.link(v.tensor_tensor(mv[:, :, 1], mv[:, :, 1], bh[:, :], ALU.add))


def hold(eng, sem):
    eng.sem_inc(sem, 1)


def token_phase(nc, B, io, scr, outer):
    ctx = ExitStack()
    with ctx:
        def sb(name, shape, dt=F32):
            return ctx.enter_context(nc.sbuf_tensor(name, shape, dt))

        sem = outer["sem"]
        K = outer["K"]
        lists = outer["lists"]
        ident = K[:, C_ID:C_ID + 128]
        identH = K[0:H, C_ID:C_ID + H]
        onesH = K[0:H, C_ONE:C_ONE + H]
        table = scr["table"]
        logits = scr["logits"]

        WG = sb("WG", [C, MAPS])
        WGc = sb("WGc", [C, MAPS])
        Wqkv = sb("Wqkv", [C, 3 * C])
        Wo = sb("Wo", [C, C])
        W1 = sb("W1", [C, 2 * C])
        W2 = sb("W2", [C, 2, C])
        brow = sb("brow", [128, 7, C])
        bcol = sb("bcol", [128, 5])
        bnp = sb("bnp", [128, 5])
        bna = sb("bna", [128, 4])
        eps = sb("eps", [128, 2])
        identb = sb("identb", [128, 128], BF16)

        XR = [sb(f"XR{i}", [C, 12 * H]) for i in range(2)]
        big = sb("big", [128, H * C])
        XT = big[0:H, :].rearrange("p (h c) -> p h c", c=C)
        big2 = sb("big2", [128, H * MAPS])
        PG = big2[0:H, :].rearrange("p (h m) -> p h m", m=MAPS)
        ST = sb("ST", [H, H, 6])
        mean, var, r, imp, s, t0, t1, A1, Bn, gsc, neg, gt, sel, ar = [
            sb(n, [H, H]) for n in ("mean", "var", "r", "imp", "s", "t0", "t1", "A1", "Bn", "gsc", "neg", "gt", "sel", "ar")]
        lgs = [sb(f"lgs{i}", [E, 8 * H]) for i in range(2)]

        thr = sb("thr", [H, 1])
        ths = sb("ths", [H, 7])
        cmpb = sb("cmpb", [H, 7, H], BF16)
        cnt = sb("cnt", [H, 7])
        acc = sb("acc", [H, 1])
        jnk = sb("jnk", [H, 7])
        eqx = sb("eqx", [H, H + 1])
        need = sb("need", [H, 1])
        bone = sb("bone", [H, H, 6], BF16)
        sp3 = sb("sp3", [H, 3, H], BF16)
        RH = sb("RH", [H, H, 5, 6], BF16)
        aoh = [sb(f"aoh{i}", [H, AR, 128], BF16) for i in range(2)]
        base = sb("base", [128, 1])
        lst = sb("lst", [128, 30])
        pix, stok, qtok, sd, rs = [sb(n, [128, 6]) for n in ("pix", "stok", "qtok", "sd", "rs")]
        pixi = sb("pixi", [128, 6], U32)
        mv = sb("mv", [128, 6, 2])
        bs = sb("bs", [128, 6, 6])
        bh = sb("bh", [128, 6])

        mx, mr = [sb(n, [128, 48]) for n in ("mx", "mr")]
        m3 = sb("m3", [128, 3, 48], BF16)
        m3T = sb("m3T", [48, 3, 128], BF16)
        rd = sb("rd", [128, 3, 4])
        X1 = sb("X1", [128, NCH, C])
        TK = sb("TK", [128, NCH, C])
        U = sb("U", [128, NCH, C])
        TT = sb("TT", [C, 2, HALF])
        KS = sb("KS", [KROWS + 3, NH, KTOK], BF16)
        V = sb("V", [128, NCH, NH, 32])
        QS = big[0:KROWS + 3, 0:3072].bitcast(BF16).rearrange("p (h n) -> p h n", h=NH)
        PR = [big[:, 3072 + 768 * i:3840 + 768 * i].rearrange("p (a n) -> p a n", a=2) for i in range(4)]
        OE = [big[:, 6144 + 384 * i:6528 + 384 * i] for i in range(2)]
        HT = [big[:, 6912 + 768 * i:7680 + 768 * i].rearrange("p (a n) -> p a n", a=2) for i in range(2)]
        F = [big2[:, 768 * i:768 * (i + 1)] for i in range(3)]
        QP, KP = [big2[:, 2304 + 1152 * i:3456 + 1152 * i].bitcast(BF16).rearrange("p (a n) -> p a n", a=3)
                  for i in range(2)]

        PD = [outer["psum"][i] for i in range(2)]
        PS = [outer["psum2"][i] for i in range(2)]
        PO = [outer["psum"][2 + i] for i in range(2)]

        def halves(ps):
            return ps[:, :, 0:HALF]

        def thirds(ps):
            return ps[:, :, 0:HALF].rearrange("p a (t c) -> p a t c", c=C)

        def six(t):
            return t[:, :, :].rearrange("p (a t) c -> p a t c", a=2)

        wloaded = sem("wloaded")
        wsummed = sem("wsummed")
        bn_root = sem("bn_root")
        pool_ready = sem("pool_ready")
        act_own, dve_own, pool_own = sem("act_own"), sem("dve_own"), sem("pool_own")
        x_in = [sem(f"x_in{i}") for i in range(2)]
        names = """setup_done rows_ready xt_copied pg_copied var_ready sd_ready maps_scaled conv_ready
            gelu_exp_ready imp_ready cnt_ready totals_ready eq_ready eq_ranked sel_ready sel_ranked
            aoh_ready aoh_used y_rows y_stored var2_ready sd2_ready gate_factors g_scaled
            lg_ready lg_staged lg_stored0 lg_stored1 rows_known tokens_in tokens_ready tt_ps tt_ready qkv_ps
            qk_copied qk_split heads_in v_ready max_ps max_read max_split maxT_ps maxT_ready max_in
            s_ps exp_done pv_done o_copied oT_ps o_ready wo_ps u_var sd3 h_ps h_ready ff_ps x1_ready
            tok_stored sel_lg_ps sel_lg_ready sel_lg_stored""".split()
        S = {n: sem(n) for n in names}
        at = lambda k, per, n: k * per + n

        block = ctx.enter_context(nc.Block())

        @block.sync
        def _(sp):
            loads = [(K[:, :], io["const"]), (WG[:, 0:NTAP], io["conv_w"]), (WG[:, NTAP:MAPS], io["gateT"]), (Wqkv[:, :], io["wqkvT"]),
                     (Wo[:, :], io["woT"]), (W1[:, :], io["w1T"]),
                     (W2[:, :, :], io["w2T"].rearrange("(b p) c -> p b c", p=128))]
            for n, key in enumerate(("bv", "b_o", "ln1_g", "ln1_b", "b2", "ln2_g", "ln2_b")):
                loads.append((brow[:, n, :], io[key].partition_broadcast(128)))
            for n, key in enumerate(("bq", "bk", "b1a", "b1b")):
                loads.append((bcol[:, n:n + 1], io[key].rearrange("(p a) -> p a", a=1)))
            loads.append((bcol[0:E, 4:5], io["gate_b"].rearrange("(p a) -> p a", a=1)))
            for n, key in enumerate(("conv_b", "bn_g", "bn_b", "bn_m", "bn_v")):
                loads.append((bnp[:, n:n + 1], io[key].partition_broadcast(128)))
            assert len(loads) == NLOADS
            for dst, src in loads:
                sp.dma_start(dst, src).then_inc(wloaded, 16)

            with sp.Fori(0, B) as k:
                row = 0
                for t in range(10):
                    n = LAST_GROUP[t - 2] if t >= 2 else LAST_GROUP[t + 8] - GROUPS
                    sp.wait_ge(S["rows_ready"], at(k, GROUPS, GROUPS + n))
                    m = CHUNK_ROWS[t]
                    sp.dma_start(XR[t % 2][:, 0:m * H],
                                 io["x"][bass.ds(k, 1), :, row * H:(row + m) * H].rearrange("a c n -> (a c) n")
                                 ).then_inc(x_in[t % 2], 16)
                    row += m
                for b in range(5):
                    sp.wait_ge(S["y_rows"], at(k, 5, b + 1))
                    sp.dma_start(table[bass.ds(k * ROWS + b * AR * H, AR * H), :].rearrange("(h w) c -> w h c", w=H),
                                 XT[:, b * AR:(b + 1) * AR, :]).then_inc(S["y_stored"], 16)
                    sp.dma_start(scr["current"][b * AR * H:(b + 1) * AR * H, :].rearrange("(h w) c -> w h c", w=H),
                                 XT[:, b * AR:(b + 1) * AR, :]).then_inc(S["y_stored"], 16)
                for b in range(14):
                    rows = 8 if b < 13 else 6
                    sp.wait_ge(S["lg_staged"], at(k, 14, b + 1))
                    sp.dma_start(logits[bass.ds(k, 1), :, b * 8 * H:b * 8 * H + rows * H].rearrange("a e n -> (a e) n"),
                                 lgs[b % 2][:, 0:rows * H]).then_inc(S[f"lg_stored{b % 2}"], 16)
                sp.wait_ge(S["qk_split"], at(k, 1, 1))
                for g, (pq, pk) in enumerate(((0, 0), (0, 1), (1, 0), (1, 1), (0, 2), (2, 0))):
                    for h in range(NH):
                        for dst, src, part in ((QS, QP, pq), (KS, KP, pk)):
                            sp.dma_start(dst[g * HD:(g + 1) * HD, h, :], src[h * HD:(h + 1) * HD, part, :]
                                         ).then_inc(S["heads_in"], 16)
                sp.wait_ge(S["maxT_ready"], at(k, 1, 1))
                for j in range(3):
                    sp.dma_start(QS[KROWS + j:KROWS + j + 1, :, :].rearrange("p h (q n) -> p (h q) n", n=128),
                                 m3T[:, j, :]).then_inc(S["max_in"], 16)
                sp.wait_ge(S["x1_ready"], at(k, 1, 1))
                sp.dma_start(table[bass.ds(k * ROWS + NPIX, KTOK), :].rearrange("(t p) c -> p t c", p=128),
                             X1[:, :, :]).then_inc(S["tok_stored"], 16)
                sp.wait_ge(S["sel_lg_ready"], at(k, 1, 1))
                sp.dma_start(logits[bass.ds(k, 1), :, NPIX:ROWS].rearrange("a e n -> (a e) n"), F[2][0:E, :]
                             ).then_inc(S["sel_lg_stored"], 16)
            sp.wait_ge(S["y_stored"], B * 160)
            sp.wait_ge(S["lg_stored0"], B * 7 * 16)
            sp.wait_ge(S["lg_stored1"], B * 7 * 16)
            sp.wait_ge(S["tok_stored"], B * 16)
            sp.wait_ge(S["sel_lg_stored"], B * 16)

        @block.gpsimd
        def _(pool):
            with pool.Fori(0, B) as k:
                pool.wait_ge(S["gate_factors"], at(k, 1, 1))
                hold(pool, outer["pool_held"])
                for h in range(H):
                    ins = nc.gpsimd.tensor_scalar(PG[:, h, NTAP:MAPS], PG[:, h, NTAP:MAPS], gsc[:, h:h + 1],
                                                  neg[:, h:h + 1], ALU.mult, ALU.add)
                    if h % 4 == 3 or h == H - 1:
                        ins.then_inc(S["g_scaled"], 1)
                pool.wait_ge(S["rows_known"], at(k, 1, 1))
                pool.wait_ge(S["y_stored"], at(k, 160, 160))
                hold(pool, outer["pool_held"])
                for c in range(NCH):
                    pool.indirect_dma_start(X1[:, c, :], None, scr["current"][:, :],
                                            bass.IndirectOffsetOnAxis(ap=pixi[:, c:c + 1], axis=0)
                                            ).then_inc(S["tokens_in"], 16)
                    pool.indirect_dma_start(U[:, c, :], None, io["pos"][:, :],
                                            bass.IndirectOffsetOnAxis(ap=pixi[:, c:c + 1], axis=0)
                                            ).then_inc(S["tokens_in"], 16)

        @block.scalar
        def _(act):
            own = Own(act, act_own, 0, 0)
            act.wait_ge(wloaded, NLOADS * 16)
            act.wait_ge(pool_ready, 1)
            nc.scalar.activation(bna[:, 0:1], bnp[:, 4:5], ACT.Sqrt, bias=eps[:, 1:2]).then_inc(bn_root, 1)
            with act.Fori(0, B) as k:
                own = Own(act, act_own, k, ACT_PER)
                for g in range(GROUPS):
                    act.wait_ge(S["rows_ready"], at(k, GROUPS, GROUPS + g + 1))
                    n = min(4, H - 4 * g)
                    nc.scalar.activation(XT[:, 4 * g:4 * g + n, :],
                                         PD[g % 2][0:H, 0:n * C].rearrange("p (a c) -> p a c", a=n), ACT.Copy
                                         ).then_inc(S["xt_copied"], 1)
                act.wait_ge(S["var_ready"], at(k, 1, 1))
                nc.scalar.activation(t1[:, :], var[:, :], ACT.Sqrt, bias=eps[0:H, 0:1]).then_inc(S["sd_ready"], 1)
                act.wait_ge(S["conv_ready"], at(k, 1, 1))
                own.link(nc.scalar.activation(t0[:, :], PO[0][0:H, 0:H], ACT.Gelu, bias=bna[0:H, 2:3], scale=bna[0:H, 1:2]))
                nc.scalar.activation(imp[:, :], t0[:, :], ACT.Exp, scale=-1.0).then_inc(S["gelu_exp_ready"], 1)
                act.wait_ge(S["var2_ready"], at(k, 1, 1))
                nc.scalar.activation(t0[:, :], gsc[:, :], ACT.Sqrt, bias=eps[0:H, 1:2]).then_inc(S["sd2_ready"], 1)
                for q in range(LG):
                    n = 4 if q < LG - 1 else H - 4 * (LG - 1)
                    b = q // 2
                    act.wait_ge(S["lg_ready"], at(k, LG, q + 1))
                    if q % 2 == 0 and b >= 2:
                        act.wait_ge(S[f"lg_stored{b % 2}"], at(k, 7 * 16, 16 * (b // 2)))
                    ins = nc.scalar.activation(lgs[b % 2][:, (q % 2) * 4 * H:(q % 2) * 4 * H + n * H],
                                               PS[q // 2 % 2][0:E, q % 2, 0:n * H], ACT.Identity, bias=bcol[0:E, 4:5])
                    if q % 2:
                        ins.then_inc(S["lg_staged"], 1)
                act.wait_ge(S["tt_ps"], at(k, 4, 1))
                nc.scalar.activation(TT[:, :, :], halves(PS[0]), ACT.Copy).then_inc(S["tt_ready"], 1)
                act.wait_ge(S["qkv_ps"], at(k, 3, 1))
                nc.scalar.activation(F[0].rearrange("p (a n) -> p a n", a=2), halves(PS[1]), ACT.Identity, bias=bna[:, 3:4],
                                     scale=0.25).then_inc(S["qk_copied"], 1)
                act.wait_ge(S["qkv_ps"], at(k, 3, 2))
                nc.scalar.activation(F[1].rearrange("p (a n) -> p a n", a=2), halves(PS[0]), ACT.Identity, bias=bcol[:, 1:2]
                                     ).then_inc(S["qk_copied"], 1)
                for n in range(48):
                    act.wait_ge(S["s_ps"], at(k, 48, n + 1))
                    if n >= 4:
                        act.wait_ge(S["pv_done"], at(k, 24, n // 2 - 1))
                    nc.scalar.activation(PR[n % 4][:, :, :], halves(PS[n % 2]), ACT.Exp).then_inc(S["exp_done"], 1)
                    if n % 12 == 11:
                        g = n // 12
                        act.wait_ge(S["pv_done"], at(k, 24, 6 * g + 6))
                        if g >= 2:
                            act.wait_ge(S["oT_ps"], at(k, 4, g - 1))
                        nc.scalar.activation(OE[g % 2][:, :], PO[g % 2][:, 0:HALF], ACT.Copy).then_inc(S["o_copied"], 1)
                act.wait_ge(S["tt_ps"], at(k, 4, 2))
                nc.scalar.activation(TT[:, :, :], halves(PS[1]), ACT.Copy).then_inc(S["tt_ready"], 1)
                act.wait_ge(S["u_var"], at(k, 3, 1))
                nc.scalar.activation(sd[:, :], mv[:, :, 1], ACT.Sqrt, bias=eps[:, 1:2]).then_inc(S["sd3"], 1)
                act.wait_ge(S["tt_ps"], at(k, 4, 3))
                nc.scalar.activation(TT[:, :, :], halves(PS[1]), ACT.Copy).then_inc(S["tt_ready"], 1)
                for b in range(2):
                    act.wait_ge(S["h_ps"], at(k, 2, b + 1))
                    nc.scalar.activation(HT[b][:, :, :], halves(PS[b]), ACT.Relu, bias=bcol[:, 2 + b:3 + b]
                                         ).then_inc(S["h_ready"], 1)
                for n in (2, 3):
                    act.wait_ge(S["u_var"], at(k, 3, n))
                    nc.scalar.activation(sd[:, :], mv[:, :, 1], ACT.Sqrt, bias=eps[:, 1:2]).then_inc(S["sd3"], 1)
                act.wait_ge(S["tt_ps"], at(k, 4, 4))
                nc.scalar.activation(TT[:, :, :], halves(PS[1]), ACT.Copy).then_inc(S["tt_ready"], 1)
                act.wait_ge(S["sel_lg_ps"], at(k, 1, 1))
                nc.scalar.activation(F[2][0:E, :].rearrange("p (a n) -> p a n", a=2), halves(PS[0])[0:E], ACT.Identity,
                                     bias=bcol[0:E, 4:5]).then_inc(S["sel_lg_ready"], 1)
                own.pad()
                act.wait_ge(S["y_stored"], at(k, 160, 160))
                act.wait_ge(S["sel_lg_stored"], at(k, 16, 16))
                for b in range(2):
                    act.wait_ge(S[f"lg_stored{b}"], at(k, 7 * 16, 7 * 16))

        @block.vector
        def _(dve):
            v = nc.vector
            once = Own(dve, dve_own, 0, 0)
            once.step(v.memset(eps[:, 0:1], 1e-6))
            once.step(v.memset(eps[:, 1:2], 1e-5))
            once.step(v.memset(base[:, :], 0.0))
            once.step(v.memset(V[:, :, :, :], 0.0))
            once.step(v.memset(KS[KROWS:KROWS + 3, :, :], 1.0))
            dve.wait_ge(wloaded, NLOADS * 16)
            once.link(v.tensor_copy(identb[:, :], ident))
            once.link(v.memset(V[:, :, :, HD:HD + 1], 1.0))
            dve.sem_inc(pool_ready, 1)
            dve.wait_ge(wsummed, 1)
            once.link(v.scalar_tensor_tensor(WGc[:, :], PO[0][:, 0:MAPS], -1.0 / C, WG[:, :], ALU.mult, ALU.add))
            dve.wait_ge(bn_root, 1)
            once.link(v.reciprocal(bna[:, 1:2], bna[:, 0:1]))
            once.link(v.tensor_tensor(bna[:, 1:2], bna[:, 1:2], bnp[:, 1:2], ALU.mult))
            once.link(v.tensor_tensor(bna[:, 2:3], bnp[:, 0:1], bnp[:, 3:4], ALU.subtract))
            once.link(v.tensor_tensor(bna[:, 2:3], bna[:, 2:3], bna[:, 1:2], ALU.mult))
            once.link(v.tensor_tensor(bna[:, 2:3], bna[:, 2:3], bnp[:, 2:3], ALU.add))
            once.link(v.tensor_scalar(bna[:, 3:4], bcol[:, 0:1], 0.25, None, ALU.mult))
            dve.sem_inc(dve_own, DVE_PER - once.n)
            v.sem_inc(S["pg_copied"], GROUPS)
            dve.sem_inc(S["setup_done"], 1)
            with dve.Fori(0, B) as k:
                own = Own(dve, dve_own, k, DVE_PER)
                own.n = DVE_PER
                own.per = DVE_PER
                link, step = own.link, own.step
                for g in range(GROUPS):
                    dve.wait_ge(S["rows_ready"], at(k, GROUPS, GROUPS + g + 1))
                    n = min(4, H - 4 * g)
                    v.tensor_copy(PG[:, 4 * g:4 * g + n, :],
                                  PO[g % 2][0:H, 0:n * MAPS].rearrange("p (a m) -> p a m", a=n)
                                  ).then_inc(S["pg_copied"], 1)
                    dve.wait_ge(S["xt_copied"], at(k, GROUPS, g + 1))
                    for h in range(4 * g, 4 * g + n):
                        step(v.bn_stats(ST[:, h, :], XT[:, h, :]))
                own.wait()
                step(v.tensor_tensor(mean[:, :], ST[:, :, 1], ST[:, :, 4], ALU.add))
                step(v.tensor_tensor(t0[:, :], ST[:, :, 1], ST[:, :, 4], ALU.subtract))
                link(v.tensor_tensor(var[:, :], ST[:, :, 2], ST[:, :, 5], ALU.add))
                step(v.tensor_scalar(mean[:, :], mean[:, :], 0.5, None, ALU.mult))
                step(v.tensor_scalar(var[:, :], var[:, :], 1.0 / C, None, ALU.mult))
                link(v.tensor_scalar(t0[:, :], t0[:, :], 0.5, None, ALU.mult))
                link(v.tensor_tensor(t0[:, :], t0[:, :], t0[:, :], ALU.mult))
                v.tensor_tensor(var[:, :], var[:, :], t0[:, :], ALU.add).then_inc(S["var_ready"], 1)
                dve.wait_ge(S["sd_ready"], at(k, 1, 1))
                link(v.reciprocal(r[:, :], t1[:, :]))
                dve.wait_ge(S["pg_copied"], at(k, GROUPS, 2 * GROUPS))
                v.tensor_tensor(PG[:, :, 0:NTAP], PG[:, :, 0:NTAP], bc(r[:, :], [H, H, NTAP], 2), ALU.mult
                                ).then_inc(S["maps_scaled"], 1)
                dve.wait_ge(S["gelu_exp_ready"], at(k, 1, 1))
                link(v.tensor_scalar(imp[:, :], imp[:, :], 1.0, None, ALU.add))
                link(v.reciprocal(imp[:, :], imp[:, :]))
                link(v.tensor_tensor(s[:, :], r[:, :], imp[:, :], ALU.mult))
                step(v.tensor_scalar(A1[:, :], s[:, :], 1.0, None, ALU.add))
                link(v.scalar_tensor_tensor(Bn[:, :], mean[:, :], -1.0, s[:, :], ALU.mult, ALU.mult))
                link(v.tensor_tensor(t1[:, :], A1[:, :], A1[:, :], ALU.mult))
                v.tensor_tensor(gsc[:, :], t1[:, :], var[:, :], ALU.mult).then_inc(S["var2_ready"], 1)
                dve.wait_ge(S["xt_copied"], at(k, GROUPS, GROUPS))
                for h in range(H):
                    ins = v.tensor_scalar(XT[:, h, :], XT[:, h, :], A1[:, h:h + 1], Bn[:, h:h + 1], ALU.mult, ALU.add)
                    if h % AR == AR - 1:
                        ins.then_inc(S["y_rows"], 1)
                dve.wait_ge(S["sd2_ready"], at(k, 1, 1))
                link(v.reciprocal(t1[:, :], t0[:, :]))
                link(v.tensor_tensor(gsc[:, :], A1[:, :], t1[:, :], ALU.mult))

                link(v.memset(thr[:, :], 0.25))
                for i in range(SEARCH):
                    m = 7 if i < SEARCH - 1 else 1
                    u = 8.0 ** -(i + 1) if i < SEARCH - 1 else 2.0 ** -25
                    link(v.tensor_scalar(ths[:, 0:m], K[0:H, C_TH:C_TH + m], u, thr[:, 0:1], ALU.mult, ALU.add))
                    link(v.tensor_tensor(cmpb[:, 0:m, :], bc(imp[:, :], [H, m, H], 1), bc(ths[:, 0:m], [H, m, H], 2),
                                         ALU.is_ge))
                    v.tensor_reduce(cnt[:, 0:m], cmpb[:, 0:m, :], AX.X, ALU.add).then_inc(S["cnt_ready"], 1)
                    dve.wait_ge(S["totals_ready"], at(k, SEARCH, i + 1))
                    link(v.tensor_scalar(jnk[:, 0:m], PO[1][0:H, 0:m], KTOK - 0.5, None, ALU.is_ge))
                    link(v.tensor_reduce(acc[:, :], jnk[:, 0:m], AX.X, ALU.add))
                    link(v.scalar_tensor_tensor(thr[:, :], acc[:, :], u, thr[:, :], ALU.mult, ALU.add))
                step(v.tensor_scalar(eqx[:, 0:H], imp[:, :], thr[:, 0:1], None, ALU.is_equal))
                link(v.tensor_scalar(gt[:, :], imp[:, :], thr[:, 0:1], None, ALU.is_gt))
                v.tensor_reduce(eqx[:, H:H + 1], gt[:, :], AX.X, ALU.add).then_inc(S["eq_ready"], 1)
                dve.wait_ge(S["eq_ranked"], at(k, 1, 1))

                def rank():
                    step(v.tensor_copy(t0[:, :], PO[0][0:H, 0:H]))
                    link(v.tensor_copy(t1[:, :], PO[1][0:H, 0:H]))
                    link(v.tensor_tensor_scan(ar[:, :], K[0:H, C_ONE:C_ONE + H], t0[:, :], 0.0, ALU.mult, ALU.add))
                    link(v.tensor_tensor(ar[:, :], ar[:, :], t0[:, :], ALU.subtract))
                    link(v.tensor_tensor(ar[:, :], ar[:, :], t1[:, :], ALU.add))

                step(v.tensor_scalar(need[:, :], PO[0][0:H, H:H + 1], -1.0, float(KTOK), ALU.mult, ALU.add))
                rank()
                link(v.tensor_scalar(ar[:, :], ar[:, :], need[:, :], None, ALU.is_lt))
                link(v.tensor_tensor(ar[:, :], ar[:, :], eqx[:, 0:H], ALU.mult))
                v.tensor_tensor(sel[:, :], ar[:, :], gt[:, :], ALU.add).then_inc(S["sel_ready"], 1)
                dve.wait_ge(S["sel_ready"], at(k, 1, 1))
                v.tensor_scalar(neg[:, :], sel[:, :], NEG, None, ALU.mult).then_inc(S["gate_factors"], 1)
                dve.wait_ge(S["sel_ranked"], at(k, 1, 1))
                rank()
                link(v.tensor_scalar(t0[:, :], sel[:, :], -4096.0, 4096.0, ALU.mult, ALU.add))
                link(v.tensor_tensor(ar[:, :], ar[:, :], t0[:, :], ALU.add))
                link(v.tensor_tensor(cmpb[:, :, :], bc(ar[:, :], [H, 7, H], 1),
                                     bc(K[0:H, C_RAMP:C_RAMP + 7], [H, 7, H], 2), ALU.is_ge))
                step(v.tensor_tensor(bone[:, :, :].rearrange("p h b -> p b h"), cmpb[:, 0:6, :], cmpb[:, 1:7, :], ALU.subtract))
                step(v.tensor_reduce(t0[:, :], cmpb[:, 1:6, :].rearrange("p m h -> p h m"), AX.X, ALU.add))
                step(v.tensor_copy(sp3[:, 0, :], s[:, :]))
                own.wait()
                step(v.tensor_tensor(t1[:, :], s[:, :], sp3[:, 0, :], ALU.subtract))
                link(v.scalar_tensor_tensor(ar[:, :], t0[:, :], -128.0, ar[:, :], ALU.mult, ALU.add))
                link(v.tensor_copy(sp3[:, 1, :], t1[:, :]))
                link(v.tensor_tensor(sp3[:, 2, :], t1[:, :], sp3[:, 1, :], ALU.subtract))
                step(v.tensor_scalar(RH[:, :, 0, :], bone[:, :, :], K[0:H, C_W:C_W + 1], None, ALU.mult))
                step(v.tensor_tensor(RH[:, :, 1, :], bone[:, :, :], bc(K[0:H, C_HROW:C_HROW + H], [H, H, 6], 2), ALU.mult))
                for j in range(3):
                    step(v.tensor_tensor(RH[:, :, 2 + j, :], bone[:, :, :], bc(sp3[:, j, :], [H, H, 6], 2), ALU.mult))
                own.wait()
                for b in range(5):
                    if b >= 2:
                        dve.wait_ge(S["aoh_used"], at(k, 5, b - 1))
                    v.tensor_tensor(aoh[b % 2][:, :, :], bc(K[0:H, C_IOTA:C_IOTA + 128], [H, AR, 128], 1),
                                    bc(ar[:, b * AR:(b + 1) * AR], [H, AR, 128], 2), ALU.is_equal
                                    ).then_inc(S["aoh_ready"], 1)
                dve.wait_ge(S["aoh_used"], at(k, 5, 5))
                link(v.tensor_copy(lst[:, :], PD[0][:, 0:30]))
                step(v.tensor_tensor(stok[:, :], lst[:, 12:18], lst[:, 18:24], ALU.add))
                link(v.scalar_tensor_tensor(pix[:, :], lst[:, 6:12], float(H), lst[:, 0:6], ALU.mult, ALU.add))
                step(v.tensor_copy(pixi[:, :], pix[:, :]))
                step(v.tensor_scalar(pix[:, :], pix[:, :], base[:, 0:1], None, ALU.add))
                link(v.tensor_tensor(stok[:, :], stok[:, :], lst[:, 24:30], ALU.add))
                step(v.tensor_scalar(base[:, :], base[:, :], float(ROWS), None, ALU.add))
                v.tensor_copy(lists[:, bass.ds(k * 6, 6)], pix[:, :]).then_inc(S["rows_known"], 1)

                link(v.tensor_scalar(rs[:, :], stok[:, :], 1.0, None, ALU.add))
                link(v.reciprocal(rs[:, :], rs[:, :]))
                link(v.tensor_tensor(qtok[:, :], rs[:, :], stok[:, :], ALU.mult))
                dve.wait_ge(S["tokens_in"], at(k, 192, 192))

                def stats(src):
                    for c in range(NCH):
                        step(v.bn_stats(bs[:, c, :], src[:, c, :]))
                    own.wait()
                    combine(v, own, mv, bs, bh)

                stats(X1)
                for c in range(NCH):
                    step(v.tensor_scalar(TK[:, c, :], X1[:, c, :], mv[:, c, 0:1], qtok[:, c:c + 1], ALU.subtract, ALU.mult))
                own.wait()
                step(v.tensor_tensor(X1[:, :, :], X1[:, :, :], TK[:, :, :], ALU.subtract))
                own.wait()
                v.tensor_tensor(TK[:, :, :], TK[:, :, :], U[:, :, :], ALU.add).then_inc(S["tokens_ready"], 1)
                for n, parts in ((0, QP), (1, KP)):
                    dve.wait_ge(S["qk_copied"], at(k, 2, n + 1))
                    link(v.tensor_copy(parts[:, 0, :], F[n]))
                    link(v.tensor_tensor(F[2], F[n], parts[:, 0, :], ALU.subtract))
                    link(v.tensor_copy(parts[:, 1, :], F[2]))
                    ins = v.tensor_tensor(parts[:, 2, :], F[2], parts[:, 1, :], ALU.subtract)
                    if n == 0:
                        link(ins)
                    else:
                        ins.then_inc(S["qk_split"], 1)
                dve.wait_ge(S["qkv_ps"], at(k, 3, 3))
                v.tensor_tensor(V[:, :, :, 0:HD].rearrange("p (a t) h d -> p a t h d", a=2),
                                thirds(PS[1]).rearrange("p a t (h d) -> p a t h d", d=HD),
                                bc(bc(brow[:, 0, :], [128, 3, C], 1), [128, 2, 3, C], 1).rearrange(
                                    "p a t (h d) -> p a t h d", d=HD), ALU.add).then_inc(S["v_ready"], 1)
                for n in range(48):
                    dve.wait_ge(S["max_ps"], at(k, 48, n + 1))
                    v.tensor_reduce(mx[:, n:n + 1], halves(PS[n % 2]), AX.XY, ALU.max).then_inc(S["max_read"], 1)
                dve.wait_ge(S["max_read"], at(k, 48, 48))
                link(v.tensor_scalar(mx[:, :], mx[:, :], -1.0, None, ALU.mult))
                link(v.tensor_copy(m3[:, 0, :], mx[:, :]))
                link(v.tensor_tensor(mr[:, :], mx[:, :], m3[:, 0, :], ALU.subtract))
                link(v.tensor_copy(m3[:, 1, :], mr[:, :]))
                v.tensor_tensor(m3[:, 2, :], mr[:, :], m3[:, 1, :], ALU.subtract).then_inc(S["max_split"], 1)
                dve.wait_ge(S["maxT_ps"], at(k, 1, 1))
                v.tensor_copy(m3T[:, :, :], PO[0][0:48, :].bitcast(BF16)[:, 0:384].rearrange("p (a n) -> p a n", a=3)
                              ).then_inc(S["maxT_ready"], 1)
                for g in range(4):
                    dve.wait_ge(S["oT_ps"], at(k, 4, g + 1))
                    hg, half = g // 2, g % 2
                    pv = PD[g % 2][:, 0:HALF].rearrange("p (t j d) -> p t j d", t=3, d=32)
                    if g:
                        dve.wait_ge(S["o_ready"], at(k, 4, g))
                    link(v.reciprocal(rd[:, :, :], pv[:, :, :, HD]))
                    v.tensor_tensor(U[:, 3 * half:3 * half + 3, 64 * hg:64 * hg + 64].rearrange("p t (j d) -> p t j d", d=HD),
                                    pv[:, :, :, 0:HD], bc(rd[:, :, :], [128, 3, 4, HD], 3), ALU.mult
                                    ).then_inc(S["o_ready"], 1)

                def norm(gi, n):
                    stats(U)
                    dve.sem_inc(S["u_var"], 1)
                    dve.wait_ge(S["sd3"], at(k, 3, n))
                    link(v.reciprocal(rs[:, :], sd[:, :]))
                    for c in range(NCH):
                        step(v.tensor_scalar(U[:, c, :], U[:, c, :], mv[:, c, 0:1], rs[:, c:c + 1], ALU.subtract, ALU.mult))
                    own.wait()
                    if gi is not None:
                        link(v.tensor_tensor(U[:, :, :], U[:, :, :], bc(brow[:, gi, :], [128, NCH, C], 1), ALU.mult))

                dve.wait_ge(S["wo_ps"], at(k, 1, 1))
                link(v.tensor_tensor(six(U), thirds(PS[0]), six(TK), ALU.add))
                link(v.tensor_tensor(U[:, :, :], U[:, :, :], bc(brow[:, 1, :], [128, NCH, C], 1), ALU.add))
                norm(2, 1)
                v.tensor_tensor(TK[:, :, :], U[:, :, :], bc(brow[:, 3, :], [128, NCH, C], 1), ALU.add
                                ).then_inc(S["tokens_ready"], 1)
                dve.wait_ge(S["tokens_ready"], at(k, 3, 2))
                dve.wait_ge(S["ff_ps"], at(k, 1, 1))
                link(v.tensor_tensor(six(U), thirds(PS[0]), six(TK), ALU.add))
                link(v.tensor_tensor(U[:, :, :], U[:, :, :], bc(brow[:, 4, :], [128, NCH, C], 1), ALU.add))
                norm(5, 2)
                link(v.tensor_tensor(U[:, :, :], U[:, :, :], bc(brow[:, 6, :], [128, NCH, C], 1), ALU.add))
                link(v.tensor_tensor(U[:, :, :], U[:, :, :], X1[:, :, :], ALU.add))
                v.tensor_copy(X1[:, :, :], U[:, :, :]).then_inc(S["x1_ready"], 1)
                norm(None, 3)
                dve.sem_inc(S["tokens_ready"], 1)
                dve.wait_ge(S["tok_stored"], at(k, 16, 16))
                dve.wait_ge(S["sel_lg_stored"], at(k, 16, 16))
                own.n -= DVE_PER
                own.pad()

        @block.tensor
        def _(pe):
            t = nc.tensor
            pe.sem_inc(S["rows_ready"], GROUPS)
            pe.wait_ge(wloaded, NLOADS * 16)
            t.matmul(PO[0][:, 0:MAPS], K[:, C_ONE:C_ONE + 128], WG[:, :], start=True, stop=True).then_inc(wsummed, 1)
            pe.wait_ge(S["setup_done"], 1)
            with pe.Fori(0, B) as k:
                g = 0
                for c in range(10):
                    pe.wait_ge(x_in[c % 2], at(k, 80, 16 * (c // 2 + 1)))
                    for i in range(0, CHUNK_ROWS[c], 4):
                        if g >= 2:
                            pe.wait_ge(S["xt_copied"], at(k, GROUPS, g - 1))
                        pe.wait_ge(S["pg_copied"], at(k, GROUPS, g - 1 + GROUPS))
                        for j in range(min(4, H - 4 * g)):
                            xs = XR[c % 2][:, (i + j) * H:(i + j + 1) * H]
                            t.transpose(PD[g % 2][0:H, j * C:(j + 1) * C], xs, ident)
                            ins = t.matmul(PO[g % 2][0:H, j * MAPS:(j + 1) * MAPS], xs, WGc[:, :], start=True, stop=True)
                        ins.then_inc(S["rows_ready"], 1)
                        g += 1
                pe.wait_ge(S["maps_scaled"], at(k, 1, 1))
                order = [3, 0, 1, 2, 4, 5, 6]
                for i in order:
                    d = DIL * i - PAD
                    lo, hi = max(0, -d), min(H, H - d)
                    for j in range(TAPS):
                        ins = t.matmul(PO[0][0:H, lo:hi], K[0:H, C_SH + j * H:C_SH + (j + 1) * H],
                                       PG[:, lo + d:hi + d, i * TAPS + j], start=(i == 3 and j == 0),
                                       stop=(i == 6 and j == TAPS - 1))
                ins.then_inc(S["conv_ready"], 1)
                for i in range(SEARCH):
                    m = 7 if i < SEARCH - 1 else 1
                    pe.wait_ge(S["cnt_ready"], at(k, SEARCH, i + 1))
                    t.matmul(PO[1][0:H, 0:m], onesH, cnt[:, 0:m], start=True, stop=True).then_inc(S["totals_ready"], 1)
                for ready, mask, n, ranked in (("eq_ready", eqx, H + 1, "eq_ranked"), ("sel_ready", sel, H, "sel_ranked")):
                    pe.wait_ge(S[ready], at(k, 1, 1))
                    t.matmul(PO[0][0:H, 0:n], onesH, mask[:, 0:n], start=True, stop=True)
                    t.matmul(PO[1][0:H, 0:H], K[0:H, C_LT:C_LT + H], mask[:, 0:H], start=True, stop=True
                             ).then_inc(S[ranked], 1)
                for b in range(5):
                    pe.wait_ge(S["aoh_ready"], at(k, 5, b + 1))
                    for i in range(AR):
                        h = b * AR + i
                        ins = t.matmul(PD[0][:, 0:30], aoh[b % 2][:, i, :], RH[:, h, :, :].rearrange("p a b -> p (a b)"),
                                       start=(h == 0), stop=(h == H - 1))
                    ins.then_inc(S["aoh_used"], 1)
                for q in range(LG):
                    n = 4 if q < LG - 1 else H - 4 * (LG - 1)
                    pe.wait_ge(S["g_scaled"], at(k, LG, q + 1))
                    if q >= 4:
                        pe.wait_ge(S["lg_staged"], at(k, 14, q // 2 - 1))
                    hold(pe, outer["pe_held"])
                    for i in range(n):
                        ins = t.transpose(PS[q // 2 % 2][0:E, q % 2, i * H:(i + 1) * H], PG[:, 4 * q + i, NTAP:MAPS], identH)
                    ins.then_inc(S["lg_ready"], 1)
                pe.wait_ge(S["lg_staged"], at(k, 14, 14))

                def turn(src, ps, ready, n):
                    for c in range(NCH):
                        ins = t.transpose(ps[:, c // 3, (c % 3) * 128:(c % 3) * 128 + 128], src[:, c, :], ident)
                    ins.then_inc(ready, n)

                def project(ps, w, inc):
                    for a in range(2):
                        ins = t.matmul(ps[0:w.shape[1], a, 0:HALF], w, TT[:, a, :], start=True, stop=True)
                    ins.then_inc(inc, 1)

                pe.wait_ge(S["tokens_ready"], at(k, 3, 1))
                turn(TK, PS[0], S["tt_ps"], 1)
                pe.wait_ge(S["tt_ready"], at(k, 4, 1))
                project(PS[1], Wqkv[:, 0:C], S["qkv_ps"])
                project(PS[0], Wqkv[:, C:2 * C], S["qkv_ps"])
                pe.wait_ge(S["qk_copied"], at(k, 2, 1))
                for c in range(NCH):
                    ins = t.matmul(PS[1][:, c // 3, (c % 3) * 128:(c % 3) * 128 + 128],
                                   TT[:, c // 3, (c % 3) * 128:(c % 3) * 128 + 128], Wqkv[:, 2 * C:3 * C], start=True, stop=True)
                ins.then_inc(S["qkv_ps"], 1)
                pe.wait_ge(S["heads_in"], at(k, 96 * 16, 96 * 16))
                pe.wait_ge(S["qk_copied"], at(k, 2, 2))
                pe.wait_ge(S["v_ready"], at(k, 1, 1))
                for n in range(48):
                    h, q = n // 6, n % 6
                    if n >= 2:
                        pe.wait_ge(S["max_read"], at(k, 48, n - 1))
                    for a in range(2):
                        ins = t.matmul(PS[n % 2][:, a, 0:HALF], QS[0:KROWS, h, q * 128:(q + 1) * 128],
                                       KS[0:KROWS, h, a * HALF:(a + 1) * HALF], start=True, stop=True)
                    ins.then_inc(S["max_ps"], 1)
                pe.wait_ge(S["max_split"], at(k, 1, 1))
                hold(pe, outer["pe_held"])
                for j in range(3):
                    ins = t.transpose(PO[0][0:48, :].bitcast(BF16)[:, 128 * j:128 * j + 128], m3[:, j, :], identb[:, :])
                ins.then_inc(S["maxT_ps"], 1)
                pe.wait_ge(S["max_in"], at(k, 48, 48))

                def weigh(m):
                    g, kc = m // 6, m % 6
                    pe.wait_ge(S["exp_done"], at(k, 48, 2 * m + 2))
                    if kc == 0 and g >= 2:
                        pe.wait_ge(S["o_copied"], at(k, 4, g - 1))
                    for j in range(4):
                        ins = t.matmul(PO[g % 2][32 * j:32 * j + 32, 0:HALF], V[:, kc, 4 * (g // 2) + j, :],
                                       PR[(2 * m + j // 2) % 4][:, j % 2, :], start=(kc == 0), stop=(kc == NCH - 1))
                    ins.then_inc(S["pv_done"], 1)

                def turn_heads(g):
                    pe.wait_ge(S["o_copied"], at(k, 4, g + 1))
                    if g >= 2:
                        pe.wait_ge(S["o_ready"], at(k, 4, g - 1))
                    for c in range(3):
                        ins = t.transpose(PD[g % 2][:, c * 128:(c + 1) * 128], OE[g % 2][:, c * 128:(c + 1) * 128], ident)
                    ins.then_inc(S["oT_ps"], 1)

                for n in range(48):
                    m = n // 2
                    g, kc = m // 6, m % 6
                    half = g % 2
                    if n >= 2:
                        pe.wait_ge(S["exp_done"], at(k, 48, n - 1))
                    for a in range(2):
                        h = 4 * (g // 2) + 2 * (n % 2) + a
                        ins = t.matmul(PS[n % 2][:, a, 0:HALF], KS[:, h, kc * 128:(kc + 1) * 128],
                                       QS[:, h, half * HALF:(half + 1) * HALF], start=True, stop=True)
                    ins.then_inc(S["s_ps"], 1)
                    if n % 2 and m >= 1:
                        weigh(m - 1)
                        if m % 6 == 2 and m >= 8:
                            turn_heads(m // 6 - 1)
                weigh(23)
                turn_heads(3)
                pe.wait_ge(S["o_ready"], at(k, 4, 4))
                turn(U, PS[1], S["tt_ps"], 1)
                pe.wait_ge(S["tt_ready"], at(k, 4, 2))
                for c in range(NCH):
                    ins = t.matmul(PS[0][:, c // 3, (c % 3) * 128:(c % 3) * 128 + 128],
                                   TT[:, c // 3, (c % 3) * 128:(c % 3) * 128 + 128], Wo[:, :], start=True, stop=True)
                ins.then_inc(S["wo_ps"], 1)
                pe.wait_ge(S["tokens_ready"], at(k, 3, 2))
                turn(TK, PS[1], S["tt_ps"], 1)
                pe.wait_ge(S["tt_ready"], at(k, 4, 3))
                project(PS[0], W1[:, 0:C], S["h_ps"])
                project(PS[1], W1[:, C:2 * C], S["h_ps"])
                pe.wait_ge(S["h_ready"], at(k, 2, 2))
                for c in range(NCH):
                    for b in range(2):
                        ins = t.matmul(PS[0][:, c // 3, (c % 3) * 128:(c % 3) * 128 + 128],
                                       HT[b][:, c // 3, (c % 3) * 128:(c % 3) * 128 + 128], W2[:, b, :],
                                       start=(b == 0), stop=(b == 1))
                ins.then_inc(S["ff_ps"], 1)
                pe.wait_ge(S["tokens_ready"], at(k, 3, 3))
                turn(U, PS[1], S["tt_ps"], 1)
                pe.wait_ge(S["tt_ready"], at(k, 4, 4))
                project(PS[0], WG[:, NTAP:MAPS], S["sel_lg_ps"])
                pe.wait_ge(S["sel_lg_ready"], at(k, 1, 1))


def pick_phase(nc, B, io, scr, outer):
    ctx = ExitStack()
    with ctx:
        def sb(name, shape, dt=F32):
            return ctx.enter_context(nc.sbuf_tensor(name, shape, dt))

        sem = outer["sem"]
        K, topv, rows, PT = outer["K"], outer["topv"], outer["rows"], outer["PT"]
        L = [sb(f"L{u}", [128, ROWS]) for u in range(2)]
        ex = sb("ex", [128, ROWS], BF16)
        mval, pv8, pbase, eps5 = sb("mval", [128, TOPE]), sb("pv8", [128, TOPE]), sb("pbase", [128, 1]), sb("eps5", [128, 1])
        nmax, z, rz = sb("nmax", [128, 1]), sb("z", [128, 1]), sb("rz", [128, 1])
        mi = sb("mi", [128, TOPE], U32)
        ri = sb("ri", [128, TOPE], U32)
        rf = sb("rf", [128, TOPE])
        XG = sb("XG", [128, TOPE, C])
        XN = sb("XN", [128, TOPE, C])
        bs = sb("pbs", [128, TOPE, 6])
        bh = sb("pbh", [128, TOPE])
        mv = sb("pmv", [128, TOPE, 2])
        sd, rs = sb("psd", [128, TOPE]), sb("prs", [128, TOPE])
        pooled = sb("pooled", [128, C])
        ps = outer["psum"][0]
        own_sem = sem("pick_own")
        S = {n: sem("pick_" + n) for n in """l_in max_ready exp_done idx_ready rows_in kept var_ready sd_ready
            pooled_ready turned pair_done""".split()}
        at = lambda k, per, n: k * per + n
        PER = 60
        block = ctx.enter_context(nc.Block())

        @block.sync
        def _(sp):
            sp.sem_inc(S["pair_done"], 2)
            with sp.Fori(0, B // 4) as j:
              for u in range(2):
                i = j * 2 + u
                sp.wait_ge(S["pair_done"], at(i, 1, 1))
                sp.dma_start(L[u][:, :],
                             scr["logits"][bass.ds(i * 2, 2), :, :].rearrange("a e n -> (a e) n")).then_inc(S["l_in"], 16)
                sp.wait_ge(S["l_in"], at(i, 16, 16))
                hold(sp, outer["sp_held"])

        @block.gpsimd
        def _(pool):
            with pool.Fori(0, B // 4) as j:
              for u in range(2):
                i = j * 2 + u
                pool.wait_ge(S["idx_ready"], at(i, 1, 1))
                hold(pool, outer["pool_held"])
                for n in range(TOPE):
                    pool.indirect_dma_start(XG[:, n, :], None, scr["table"][:, :],
                                            bass.IndirectOffsetOnAxis(ap=ri[:, n:n + 1], axis=0)
                                            ).then_inc(S["rows_in"], 16)
                pool.wait_ge(S["rows_in"], at(i, 16 * TOPE, 16 * TOPE))
                hold(pool, outer["pool_held"])
                pool.dma_start(scr["picked"][bass.ds(i * 128, 128), :], XG[:, :, :].rearrange("p k c -> p (k c)")
                               ).then_inc(S["kept"], 16)
            pool.wait_ge(S["kept"], 16 * (B // 2))

        @block.scalar
        def _(act):
            with act.Fori(0, B // 4) as j:
              for u in range(2):
                i = j * 2 + u
                act.wait_ge(S["max_ready"], at(i, 1, 1))
                nc.scalar.activation(pv8[:, :], mval[:, :], ACT.Exp, bias=nmax[:, 0:1])
                nc.scalar.activation(ex[:, :], L[u][:, :], ACT.Exp, bias=nmax[:, 0:1],
                                     accum_out=z[:, 0:1]).then_inc(S["exp_done"], 1)
                act.wait_ge(S["var_ready"], at(i, 1, 1))
                nc.scalar.activation(sd[:, :], mv[:, :, 1], ACT.Sqrt, bias=eps5[:, 0:1]).then_inc(S["sd_ready"], 1)
                act.wait_ge(S["exp_done"], at(i, 1, 1))

        @block.vector
        def _(dve):
            v = nc.vector
            once = Own(dve, own_sem, 0, PER)
            once.step(v.memset(eps5[:, :], 1e-5))
            once.link(v.tensor_copy(pbase[:, :], K[:, C_S1:C_S1 + 1]))
            once.pad()
            with dve.Fori(0, B // 4) as j:
              for u in range(2):
                i = j * 2 + u
                own = Own(dve, own_sem, i, PER)
                own.n = PER
                link, step = own.link, own.step
                Li = L[u][:, :]
                dve.wait_ge(S["l_in"], at(i, 16, 16))
                hold(dve, outer["dve_held"])
                link(v.max(mval[:, :], Li))
                v.tensor_scalar(nmax[:, :], mval[:, 0:1], -1.0, None, ALU.mult).then_inc(S["max_ready"], 1)
                link(v.max_index(mi[:, :], mval[:, :], Li))
                link(v.tensor_copy(rf[:, :], mi[:, :]))
                link(v.tensor_scalar(rf[:, :], rf[:, :], pbase[:, 0:1], None, ALU.add))
                step(v.tensor_scalar(pbase[:, :], pbase[:, :], 2.0 * ROWS, None, ALU.add))
                step(v.tensor_copy(rows[:, bass.ds(i * TOPE, TOPE)], rf[:, :]))
                v.tensor_copy(ri[:, :], rf[:, :]).then_inc(S["idx_ready"], 1)
                dve.wait_ge(S["exp_done"], at(i, 1, 1))
                link(v.reciprocal(rz[:, :], z[:, :]))
                link(v.tensor_scalar(pv8[:, :], pv8[:, :], rz[:, 0:1], None, ALU.mult))
                step(v.tensor_copy(topv[:, bass.ds(i * TOPE, TOPE)], pv8[:, :]))
                dve.wait_ge(S["rows_in"], at(i, 16 * TOPE, 16 * TOPE))
                for n in range(TOPE):
                    step(v.bn_stats(bs[:, n, :], XG[:, n, :]))
                own.wait()
                combine(v, own, mv, bs, bh)
                dve.sem_inc(S["var_ready"], 1)
                dve.wait_ge(S["sd_ready"], at(i, 1, 1))
                link(v.reciprocal(rs[:, :], sd[:, :]))
                link(v.tensor_tensor(rs[:, :], rs[:, :], pv8[:, :], ALU.mult))
                for n in range(TOPE):
                    step(v.tensor_scalar(XN[:, n, :], XG[:, n, :], mv[:, n, 0:1], rs[:, n:n + 1], ALU.subtract, ALU.mult))
                own.wait()
                v.tensor_reduce(pooled[:, :], XN[:, :, :].rearrange("p k c -> p c k"), AX.X, ALU.add
                                ).then_inc(S["pooled_ready"], 1)
                dve.wait_ge(S["turned"], at(i, 1, 1))
                v.tensor_copy(PT[:, bass.ds(i * 128, 128)], ps[:, 0:128]).then_inc(S["pair_done"], 1)
                own.n -= PER
                own.pad()
                dve.wait_ge(S["kept"], at(i, 16, 16))

        @block.tensor
        def _(pe):
            with pe.Fori(0, B // 4) as j:
              for u in range(2):
                i = j * 2 + u
                pe.wait_ge(S["pooled_ready"], at(i, 1, 1))
                nc.tensor.transpose(ps[:, 0:128], pooled[:, :], K[:, C_ID:C_ID + 128]).then_inc(S["turned"], 1)


def expert_phase(nc, B, io, scr, outer):
    ctx = ExitStack()
    with ctx:
        def sb(name, shape, dt=F32):
            return ctx.enter_context(nc.sbuf_tensor(name, shape, dt))

        sem = outer["sem"]
        K, PT = outer["K"], outer["PT"]
        PTv = PT[:, :].rearrange("d (b e) -> d e b", e=E)
        W1S = [sb(f"W1S{i}", [C, 4, HID]) for i in range(2)]
        W1B = [sb(f"W1B{i}", [1, 4, HID]) for i in range(2)]
        W2S = [sb(f"W2S{i}", [128, 4, 4, C]) for i in range(2)]
        W2B = [sb(f"W2B{i}", [1, 4, C]) for i in range(2)]
        PTE = [sb(f"PTE{i}", [C, 4, 32]) for i in range(2)]
        HS = [sb(f"HS{i}", [128, HID]) for i in range(2)]
        HST = [sb(f"HST{i}", [128, 4, 128]) for i in range(2)]
        OS = [sb(f"OS{i}", [128, C]) for i in range(2)]
        psH = [outer["psum"][i] for i in range(2)]
        psT = [outer["psum"][2 + i] for i in range(2)]
        psO = [outer["psum2"][i][:, 0, :] for i in range(2)]
        w_in = [sem(f"w_in{i}") for i in range(2)]
        S = {n: sem("ex_" + n) for n in "zeroed picked h_ps h_ready hT_ps hT_ready o_ps o_ready stored0 stored1".split()}
        at = lambda k, per, n: k * per + n
        block = ctx.enter_context(nc.Block())
        NG = E // 4

        @block.sync
        def _(sp):
            sp.sem_inc(S["o_ps"], 2)
            with sp.Fori(0, NG // 2) as i:
                for u in range(2):
                    sp.wait_ge(S["o_ps"], at(i, 2, u + 1))
                    e = i * 8 + 4 * u
                    sp.dma_start(W1S[u][:, :, :], io["weight1"][bass.ds(e, 4), 0:C, :].rearrange("e d n -> d e n")
                                 ).then_inc(w_in[u], 16)
                    sp.dma_start(W1B[u][:, :, :], io["weight1"][bass.ds(e, 4), C:C + 1, :].rearrange("e d n -> d e n")
                                 ).then_inc(w_in[u], 16)
                    for c in range(4):
                        sp.dma_start(W2S[u][:, :, c, :], io["weight2"][bass.ds(e, 4), c * 128:(c + 1) * 128, :].rearrange(
                            "e p n -> p e n")).then_inc(w_in[u], 16)
                    sp.dma_start(W2B[u][:, :, :], io["weight2"][bass.ds(e, 4), HID:HID + 1, :].rearrange("e d n -> d e n")
                                 ).then_inc(w_in[u], 16)

        @block.gpsimd
        def _(pool):
            with pool.Fori(0, NG // 2) as i:
                for u in range(2):
                    pool.wait_ge(S["o_ready"], at(i, 2, u + 1))
                    hold(pool, outer["pool_held"])
                    for j in range(4):
                        pool.dma_start(scr["expert_out"][:, bass.ds(i * 8 + 4 * u + j, 1), :].rearrange("b a c -> b (a c)"),
                                       OS[u][32 * j:32 * j + B, :]).then_inc(S[f"stored{u}"], 16)
            for u in range(2):
                pool.wait_ge(S[f"stored{u}"], NG // 2 * 64)

        @block.vector
        def _(dve):
            v = nc.vector
            for u in range(2):
                v.memset(PTE[u][:, :, :], 0.0).then_inc(S["zeroed"], 1)
            dve.wait_ge(S["zeroed"], 2)
            with dve.Fori(0, NG // 2) as i:
                for u in range(2):
                    dve.wait_ge(S["o_ps"], at(i, 2, u + 1))
                    v.tensor_copy(PTE[u][:, :, 0:B], PTv[:, bass.ds(i * 8 + 4 * u, 4), :]).then_inc(S["picked"], 1)
                for u in range(2):
                    dve.wait_ge(S["hT_ps"], at(i, 2, u + 1))
                    v.tensor_copy(HST[u][:, :, :], psT[u][:, :].rearrange("p (c n) -> p c n", c=4)).then_inc(S["hT_ready"], 1)
                    dve.wait_ge(S["o_ps"], at(i, 2, u + 3))
                    v.tensor_copy(OS[u][:, :], psO[u][:, 0:C]).then_inc(S["o_ready"], 1)
                for u in range(2):
                    dve.wait_ge(S[f"stored{u}"], at(i, 64, 64))

        @block.scalar
        def _(act):
            with act.Fori(0, NG // 2) as i:
                for u in range(2):
                    act.wait_ge(S["h_ps"], at(i, 2, u + 1))
                    nc.scalar.activation(HS[u][:, :], psH[u][:, :], ACT.Gelu).then_inc(S["h_ready"], 1)

        @block.tensor
        def _(pe):
            t = nc.tensor
            ones = K[0:1, C_ONE:C_ONE + 32]
            with pe.Fori(0, NG // 2) as i:
                for u in range(2):
                    pe.wait_ge(w_in[u], at(i, 7 * 16, 7 * 16))
                    pe.wait_ge(S["picked"], at(i, 2, u + 1))
                    for j in range(4):
                        t.matmul(psH[u][32 * j:32 * j + 32, :], PTE[u][:, j, :], W1S[u][:, j, :], start=True, stop=False)
                    for j in range(4):
                        ins = t.matmul(psH[u][32 * j:32 * j + 32, :], ones, W1B[u][:, j, :], start=False, stop=True)
                    ins.then_inc(S["h_ps"], 1)
                for u in range(2):
                    pe.wait_ge(S["h_ready"], at(i, 2, u + 1))
                    for c in range(4):
                        ins = t.transpose(psT[u][:, c * 128:(c + 1) * 128], HS[u][:, c * 128:(c + 1) * 128],
                                          K[:, C_ID:C_ID + 128])
                    ins.then_inc(S["hT_ps"], 1)
                    pe.wait_ge(S["hT_ready"], at(i, 2, u + 1))
                    for c in range(4):
                        for j in range(4):
                            t.matmul(psO[u][32 * j:32 * j + 32, 0:C], HST[u][:, c, 32 * j:32 * j + 32], W2S[u][:, j, c, :],
                                     start=(c == 0), stop=False)
                    for j in range(4):
                        ins = t.matmul(psO[u][32 * j:32 * j + 32, 0:C], ones, W2B[u][:, j, :], start=False, stop=True)
                    ins.then_inc(S["o_ps"], 1)
                pe.wait_ge(S["o_ready"], at(i, 2, 2))


def scatter_phase(nc, B, io, scr, outer):
    ctx = ExitStack()
    with ctx:
        def sb(name, shape, dt=F32):
            return ctx.enter_context(nc.sbuf_tensor(name, shape, dt))

        sem = outer["sem"]
        K, topv, rows, lists = outer["K"], outer["topv"], outer["rows"], outer["lists"]
        table = scr["table"]
        OE = sb("sOE", [128, C])
        XG = sb("sXG", [128, TOPE, C])
        WK = sb("WK", [128, TOPE, C])
        DG = sb("DG", [128, TOPE, 128])
        IR = sb("IR", [128, TOPE, 128])
        EQ = sb("EQ", [128, TOPE, TOPE, 128])
        EL = sb("EL", [128, TOPE, 128])
        rk, tv, dup = sb("rk", [128, TOPE]), sb("tv", [128, TOPE]), sb("dup", [128, TOPE])
        ri = sb("sri", [128, TOPE], U32)
        T6 = [sb(f"T6{s}", [128, NCH, C]) for s in range(2)]
        li = sb("li", [128, 2 * NCH], U32)
        own_sem = sem("sc_own")
        S = {n: sem("sc_" + n) for n in """loaded diag_ready spread_ps eq_ready sums_ps rows_ready scattered
            tokens_in tokens_out""".split()}
        at = lambda k, per, n: k * per + n
        PER = 60
        psA = outer["psum2"][0]
        psB = outer["psum2"][1]
        psC = outer["psum"][0]
        block = ctx.enter_context(nc.Block())

        @block.sync
        def _(sp):
            with sp.Fori(0, B // 2) as i:
                sp.dma_start(OE[:, :], scr["expert_out"][bass.ds(i * 2, 2), :, :].rearrange("a e c -> (a e) c")
                             ).then_inc(S["loaded"], 16)
                sp.dma_start(XG[:, :, :].rearrange("p k c -> p (k c)"), scr["picked"][bass.ds(i * 128, 128), :]
                             ).then_inc(S["loaded"], 16)
                sp.wait_ge(S["scattered"], at(i, 16 * TOPE, 16 * TOPE))
                for s in range(2):
                    sp.dma_start(T6[s][:, :, :], table[bass.ds(i * 2 * ROWS + s * ROWS + NPIX, KTOK), :].rearrange(
                        "(t p) c -> p t c", p=128)).then_inc(S["tokens_in"], 16)
                sp.wait_ge(S["tokens_out"], at(i, 2 * NCH * 16, 2 * NCH * 16))
                hold(sp, outer["sp_held"])

        @block.gpsimd
        def _(pool):
            with pool.Fori(0, B // 2) as i:
                pool.wait_ge(S["rows_ready"], at(i, 1, 1))
                hold(pool, outer["pool_held"])
                for n in range(TOPE):
                    pool.indirect_dma_start(table[:, :], bass.IndirectOffsetOnAxis(ap=ri[:, n:n + 1], axis=0),
                                            XG[:, n, :], None, bounds_check=B * ROWS - 1, oob_is_err=False
                                            ).then_inc(S["scattered"], 16)
                pool.wait_ge(S["tokens_in"], at(i, 32, 32))
                hold(pool, outer["pool_held"])
                for n in range(2 * NCH):
                    pool.indirect_dma_start(table[:, :], bass.IndirectOffsetOnAxis(ap=li[:, n:n + 1], axis=0),
                                            T6[n // NCH][:, n % NCH, :], None).then_inc(S["tokens_out"], 16)
            pool.wait_ge(S["scattered"], B // 2 * 16 * TOPE)
            pool.wait_ge(S["tokens_out"], B // 2 * 2 * NCH * 16)

        @block.vector
        def _(dve):
            v = nc.vector
            with dve.Fori(0, B // 2) as i:
                own = Own(dve, own_sem, i, PER)
                link, step = own.link, own.step
                step(v.tensor_copy(rk[:, :], rows[:, bass.ds(i * TOPE, TOPE)]))
                link(v.tensor_copy(tv[:, :], topv[:, bass.ds(i * TOPE, TOPE)]))
                v.tensor_tensor(DG[:, :, :], bc(K[:, C_ID:C_ID + 128], [128, TOPE, 128], 1), bc(rk[:, :], [128, TOPE, 128], 2),
                                ALU.mult).then_inc(S["diag_ready"], 1)
                dve.wait_ge(S["loaded"], at(i, 32, 32))
                for n in range(TOPE):
                    step(v.tensor_scalar(WK[:, n, :], OE[:, :], tv[:, n:n + 1], None, ALU.mult))
                dve.wait_ge(S["spread_ps"], at(i, 1, 1))
                link(v.tensor_copy(IR[:, :, :].rearrange("p (a k) n -> p a (k n)", a=2), psA[:, :, :]))
                for n in range(TOPE):
                    step(v.tensor_scalar(EQ[:, n, :, :], IR[:, :, :], rk[:, n:n + 1], None, ALU.is_equal))
                own.wait()
                for n in range(TOPE):
                    step(v.tensor_tensor(EL[:, n, :], EQ[:, n, n, :], K[:, C_LT:C_LT + 128], ALU.mult))
                own.wait()
                dve.sem_inc(S["eq_ready"], 1)
                dve.wait_ge(S["sums_ps"], at(i, 1, 1))
                link(v.tensor_tensor(XG[:, :, :].rearrange("p (a k) c -> p a (k c)", a=2),
                                     XG[:, :, :].rearrange("p (a k) c -> p a (k c)", a=2), psB[:, :, :], ALU.add))
                link(v.tensor_scalar(dup[:, :], psC[:, 0:TOPE], 0.5, FAR, ALU.is_ge, ALU.mult))
                link(v.tensor_tensor(dup[:, :], dup[:, :], rk[:, :], ALU.add))
                step(v.tensor_copy(li[:, :], lists[:, bass.ds(i * 2 * NCH, 2 * NCH)]))
                link(v.tensor_copy(ri[:, :], dup[:, :]))
                dve.sem_inc(S["rows_ready"], 1)
                own.pad()
                dve.wait_ge(S["tokens_out"], at(i, 2 * NCH * 16, 2 * NCH * 16))

        @block.tensor
        def _(pe):
            t = nc.tensor
            with pe.Fori(0, B // 2) as i:
                pe.wait_ge(S["diag_ready"], at(i, 1, 1))
                for a in range(2):
                    ins = t.matmul(psA[:, a, :], K[:, C_ONE:C_ONE + 128],
                                   DG[:, 4 * a:4 * a + 4, :].rearrange("p k n -> p (k n)"), start=True, stop=True)
                ins.then_inc(S["spread_ps"], 1)
                pe.wait_ge(S["eq_ready"], at(i, 1, 1))
                for m in range(TOPE):
                    for n in range(TOPE):
                        t.matmul(psB[:, m // 4, (m % 4) * 128:(m % 4) * 128 + 128], EQ[:, n, m, :], WK[:, n, :],
                                 start=(n == 0), stop=(n == TOPE - 1))
                for m in range(TOPE):
                    for n in range(m):
                        t.matmul(psC[:, m:m + 1], EQ[:, n, m, :], K[:, C_ONE:C_ONE + 1], start=(n == 0), stop=False)
                    ins = t.matmul(psC[:, m:m + 1], EL[:, m, :], K[:, C_ONE:C_ONE + 1], start=(m == 0), stop=True)
                ins.then_inc(S["sums_ps"], 1)


def output_phase(nc, B, io, scr, outer):
    ctx = ExitStack()
    with ctx:
        def sb(name, shape, dt=F32):
            return ctx.enter_context(nc.sbuf_tensor(name, shape, dt))

        sem = outer["sem"]
        K = outer["K"]
        NT, PX = 11, 10
        FT = [sb(f"FT{i}", [H, PX, C]) for i in range(2)]
        OT = [sb(f"OT{i}", [C, H, PX]) for i in range(2)]
        parts = [(0, 4), (4, 4), (8, 2)]
        ps = [[outer["psum2"][i][:, 0, :], outer["psum2"][i][:, 1, :], outer["psum"][i][:, :]] for i in range(2)]
        f_in = [sem(f"f_in{i}") for i in range(2)]
        f_out = [sem(f"f_out{i}") for i in range(2)]
        S = {n: sem("out_" + n) for n in "turned act_copied dve_copied".split()}
        at = lambda k, per, n: k * per + n
        block = ctx.enter_context(nc.Block())
        TWO = 2 * NT

        def table_rows(k, s, tile):
            return scr["table"][bass.ds(k * 2 * ROWS + s * ROWS + tile * H * PX, H * PX), :].rearrange(
                "(p a) c -> p a c", a=PX)

        def copies(eng, k, fn, name, mine):
            for n in range(TWO):
                eng.wait_ge(S["turned"], at(k, TWO, TWO + n + 1))
                if n >= 2:
                    eng.wait_ge(f_out[n % 2], at(k, NT * 16, 16 * (n // 2)))
                for part in mine(n):
                    a, m = parts[part]
                    ins = fn(OT[n % 2][:, :, a:a + m].rearrange("c p a -> c a p"),
                             ps[n % 2][part][:, 0:m * H].rearrange("c (a p) -> c a p", a=m))
                ins.then_inc(S[name], 1)
            for i in range(2):
                eng.wait_ge(f_out[i], at(k, NT * 16, NT * 16))

        @block.sync
        def _(sp):
            with sp.Fori(0, B // 2) as k:
                for n in range(TWO):
                    s, tile = n // NT, n % NT
                    sp.wait_ge(S["turned"], at(k, TWO, TWO + n - 1))
                    sp.dma_start(FT[n % 2][:, :, :], table_rows(k, s, tile)).then_inc(f_in[n % 2], 16)

        @block.gpsimd
        def _(pool):
            with pool.Fori(0, B // 2) as k:
                for n in range(TWO):
                    s, tile = n // NT, n % NT
                    pool.wait_ge(S["act_copied"], at(k, TWO, TWO + n + 1))
                    pool.wait_ge(S["dve_copied"], at(k, TWO, TWO + n + 1))
                    hold(pool, outer["pool_held"])
                    pool.dma_start(io["out"][bass.ds(k * 2 + s, 1), :, tile * H * PX:(tile + 1) * H * PX].rearrange(
                        "b c n -> (b c) n"), OT[n % 2][:, :, :].rearrange("c p a -> c (p a)")).then_inc(f_out[n % 2], 16)
            for i in range(2):
                pool.wait_ge(f_out[i], B // 2 * NT * 16)

        @block.scalar
        def _(act):
            act.sem_inc(S["act_copied"], TWO)
            with act.Fori(0, B // 2) as k:
                copies(act, k, lambda o, i: nc.scalar.activation(o, i, ACT.Copy), "act_copied",
                       lambda n: (0,) if n % 2 else (0, 2))

        @block.vector
        def _(dve):
            dve.sem_inc(S["dve_copied"], TWO)
            with dve.Fori(0, B // 2) as k:
                copies(dve, k, lambda o, i: nc.vector.tensor_copy(o, i), "dve_copied",
                       lambda n: (1, 2) if n % 2 else (1,))

        @block.tensor
        def _(pe):
            pe.sem_inc(S["turned"], TWO)
            with pe.Fori(0, B // 2) as k:
                for n in range(TWO):
                    pe.wait_ge(f_in[n % 2], at(k, NT * 16, 16 * (n // 2 + 1)))
                    pe.wait_ge(S["act_copied"], at(k, TWO, TWO + n - 1))
                    pe.wait_ge(S["dve_copied"], at(k, TWO, TWO + n - 1))
                    for part, (a, m) in enumerate(parts):
                        for j in range(m):
                            ins = nc.tensor.transpose(ps[n % 2][part][:, j * H:(j + 1) * H], FT[n % 2][:, a + j, :],
                                                      K[0:H, C_ID:C_ID + H])
                    ins.then_inc(S["turned"], 1)


def build(nc, B, io, scr):
    with ExitStack() as ctx:
        outer = {
            "sem": lambda name: ctx.enter_context(nc.semaphore(name)),
            "K": ctx.enter_context(nc.sbuf_tensor("K", [128, NCONST], F32)),
            "lists": ctx.enter_context(nc.sbuf_tensor("lists", [128, B * NCH], U32)),
            "topv": ctx.enter_context(nc.sbuf_tensor("topv", [128, B // 2 * TOPE], F32)),
            "rows": ctx.enter_context(nc.sbuf_tensor("rows", [128, B // 2 * TOPE], F32)),
            "psum2": [ctx.enter_context(nc.psum_tensor(f"pair{i}", [128, 2, 512], F32)) for i in range(2)],
            "psum": [ctx.enter_context(nc.psum_tensor(f"bank{i}", [128, 512], F32)) for i in range(4)],
        }
        for name in ("pool_held", "pe_held", "sp_held", "dve_held"):
            outer[name] = outer["sem"](name)
        token_phase(nc, B, io, scr, outer)
        outer["PT"] = ctx.enter_context(nc.sbuf_tensor("PT", [C, B * E], F32))
        pick_phase(nc, B, io, scr, outer)
        expert_phase(nc, B, io, scr, outer)
        scatter_phase(nc, B, io, scr, outer)
        output_phase(nc, B, io, scr, outer)


def kernel(**inputs):
    import concourse.bacc as _bacc
    from concourse.bass_utils import run_bass_kernel_spmd as _run

    def g(name):
        return np.asarray(inputs[name])

    x = g("x")
    B = x.shape[0]
    b_qkv, b1 = g("L0_conv_b_qkv"), g("L0_conv_b1")
    arrays = {
        "x": x.reshape(B, C, NPIX), "conv_w": g("L0_conv_conv_w").reshape(C, NTAP), "gateT": g("L0_ffn_gate_w").T,
        "wqkvT": g("L0_conv_w_qkv").T, "woT": g("L0_conv_w_o").T, "w1T": g("L0_conv_w1").T, "w2T": g("L0_conv_w2").T,
        "bq": b_qkv[:C], "bk": b_qkv[C:2 * C], "bv": b_qkv[2 * C:], "b_o": g("L0_conv_b_o"),
        "ln1_g": g("L0_conv_ln1_g"), "ln1_b": g("L0_conv_ln1_b"), "b1a": b1[:C], "b1b": b1[C:], "b2": g("L0_conv_b2"),
        "ln2_g": g("L0_conv_ln2_g"), "ln2_b": g("L0_conv_ln2_b"), "gate_b": g("L0_ffn_gate_b"),
        "conv_b": g("L0_conv_conv_b"), "bn_g": g("L0_conv_bn_g"), "bn_b": g("L0_conv_bn_b"),
        "bn_m": g("L0_conv_bn_m"), "bn_v": g("L0_conv_bn_v"), "weight1": g("L0_ffn_weight1"),
        "weight2": g("L0_ffn_weight2"), "const": constants(), "pos": positions(),
    }
    arrays = {n: np.ascontiguousarray(a) for n, a in arrays.items()}
    nc = _bacc.Bacc("TRN2", target_bir_lowering=False, num_devices=1)
    io = {n: nc.dram_tensor("in_" + n, a.shape, F32, kind="ExternalInput").ap() for n, a in arrays.items()}
    io["out"] = nc.dram_tensor("out", (B, C, NPIX), F32, kind="ExternalOutput").ap()
    scr = {
        "current": nc.dram_tensor("current", (NPIX, C), F32, kind="Internal").ap(),
        "table": nc.dram_tensor("table", (B * ROWS, C), F32, kind="Internal").ap(),
        "logits": nc.dram_tensor("logits", (B, E, ROWS), F32, kind="Internal").ap(),
        "picked": nc.dram_tensor("picked", (B // 2 * 128, TOPE * C), F32, kind="Internal").ap(),
        "expert_out": nc.dram_tensor("expert_out", (B, E, C), F32, kind="Internal").ap(),
    }
    build(nc, B, io, scr)
    r = _run(nc, [{"in_" + n: a for n, a in arrays.items()}], core_ids=[0])
    return r.results[0]["out"].reshape(B, C, H, H)
```

```python
import numpy as np
import concourse.bass as bass
from concourse import mybir
from contextlib import ExitStack

F32 = mybir.dt.float32
BF16 = mybir.dt.bfloat16
U32 = mybir.dt.uint32
ALU = mybir.AluOpType
ACT = mybir.ActivationFunctionType
AX = mybir.AxisListType

C = 128
H = 110
NPIX = H * H
NLOADS = 24
TAPS, DIL, PAD = 7, 5, 15
NTAP = TAPS * TAPS
KTOK = 768
NCH = KTOK // 128
HALF = KTOK // 2
NH, HD = 8, 16
SLOTS = 6
KROWS = SLOTS * HD
E = 64
TOPE = 8
HID = 512
MAPS = NTAP + E
ROWS = NPIX + KTOK
NEG = -1.0e30
FAR = 3.0e7
CHUNK_ROWS = (8,) * 13 + (6,)
NX = len(CHUNK_ROWS)
GROUPS = -(-H // 4)
LAST_GROUP = [-(-sum(CHUNK_ROWS[:t + 1]) // 4) for t in range(NX)]
SEARCH = 9
BR = 22
AR = 11
NA = H // AR
YD = 3
LG = 28
DVE_PER, ACT_PER = 800, 20

C_ID, C_ONE, C_LT, C_SH = 0, 128, 256, 384
C_IOTA = C_SH + TAPS * H
C_HROW = C_IOTA + 128
C_W = C_HROW + H
C_TH = C_W + 1
C_S1 = C_TH + 8
C_RAMP = C_S1 + 1
NCONST = C_RAMP + 7


def constants():
    c = np.zeros((128, NCONST), np.float32)
    p = np.arange(128)
    c[:, C_ID:C_ID + 128] = np.eye(128)
    c[:, C_ONE:C_ONE + 128] = 1
    c[:, C_LT:C_LT + 128] = p[:, None] < p[None]
    for j in range(TAPS):
        c[:, C_SH + j * H:C_SH + (j + 1) * H] = p[:, None] == p[None, :H] + DIL * j - PAD
    c[:, C_IOTA:C_IOTA + 128] = p[None]
    c[:, C_HROW:C_HROW + H] = p[None, :H]
    c[:, C_W] = p
    c[:, C_TH:C_TH + 7] = np.arange(1, 8)[None]
    c[:, C_S1] = (p >= E) * ROWS
    c[:, C_RAMP:C_RAMP + 7] = 128 * np.arange(7)[None]
    return c


def positions():
    pos = np.arange(NPIX, dtype=np.float32)[:, None]
    div = np.exp(np.arange(0, C, 2, dtype=np.float32) * -(np.log(10000.0) / C))
    pe = np.zeros((NPIX, C), dtype=np.float32)
    pe[:, 0::2] = np.sin(pos * div)
    pe[:, 1::2] = np.cos(pos * div)
    return pe


class Round:

    def __init__(self, eng, it):
        self.eng, self.it, self.products = eng, it, {}

    def times(self, per):
        if per not in self.products:
            p = self.it * per
            self.products[per] = p if isinstance(p, int) else self.eng.snap(p)
        return self.products[per]


class Own:

    def __init__(self, eng, sem, k, per, before=0):
        self.eng, self.sem, self.per, self.before, self.n = eng, sem, per, before, 0
        self.times = k.times if isinstance(k, Round) else lambda per: k * per

    def step(self, ins):
        ins.then_inc(self.sem, 1)
        self.n += 1

    def wait(self):
        self.eng.wait_ge(self.sem, self.times(self.per) + (self.before + self.n))

    def link(self, ins):
        self.step(ins)
        self.wait()

    def pad(self):
        assert self.n < self.per, self.n
        self.eng.sem_inc(self.sem, self.per - self.n)



def bc(ap, shape, at):
    return ap.unsqueeze(at).broadcast_to(shape)


def combine(v, own, mv, bs, bh):
    own.step(v.tensor_tensor(mv[:, :, 0], bs[:, :, 1], bs[:, :, 4], ALU.add))
    own.step(v.tensor_tensor(bh[:, :], bs[:, :, 1], bs[:, :, 4], ALU.subtract))
    own.link(v.tensor_tensor(mv[:, :, 1], bs[:, :, 2], bs[:, :, 5], ALU.add))
    own.step(v.tensor_scalar(mv[:, :, 0], mv[:, :, 0], 0.5, None, ALU.mult))
    own.step(v.tensor_scalar(mv[:, :, 1], mv[:, :, 1], 1.0 / C, None, ALU.mult))
    own.link(v.tensor_scalar(bh[:, :], bh[:, :], 0.5, None, ALU.mult))
    own.link(v.tensor_tensor(bh[:, :], bh[:, :], bh[:, :], ALU.mult))
    own.link(v.tensor_tensor(mv[:, :, 1], mv[:, :, 1], bh[:, :], ALU.add))


def hold(eng, sem):
    eng.sem_inc(sem, 1)


def token_phase(nc, B, io, scr, outer):
    ctx = ExitStack()
    with ctx:
        def sb(name, shape, dt=F32):
            return ctx.enter_context(nc.sbuf_tensor(name, shape, dt))

        sem = outer["sem"]
        K = outer["K"]
        lists = outer["lists"]
        ident = K[:, C_ID:C_ID + 128]
        identH = K[0:H, C_ID:C_ID + H]
        onesH = K[0:H, C_ONE:C_ONE + H]
        table = scr["table"]
        logits = scr["logits"]

        WG = sb("WG", [C, MAPS])
        WGc = sb("WGc", [C, MAPS])
        Wqkv = sb("Wqkv", [C, 3 * C])
        Wo = sb("Wo", [C, C])
        W1 = sb("W1", [C, 2 * C])
        W2 = sb("W2", [C, 2, C])
        brow = sb("brow", [128, 7, C])
        bcol = sb("bcol", [128, 5])
        bnp = sb("bnp", [128, 5])
        bna = sb("bna", [128, 4])
        eps = sb("eps", [128, 2])
        identb = sb("identb", [128, 128], BF16)

        XR = [sb(f"XR{i}", [C, 8 * H]) for i in range(2)]
        XT = sb("XT", [H, H, C])
        PG = sb("PG", [H, H, MAPS])
        ST = sb("ST", [H, H, 6])
        mean, var, r, imp, s, t0, t1, A1, Bn, gsc, neg, gt, sel, ar = [
            sb(n, [H, H]) for n in ("mean", "var", "r", "imp", "s", "t0", "t1", "A1", "Bn", "gsc", "neg", "gt", "sel", "ar")]

        thr = sb("thr", [H, 1])
        ths = sb("ths", [H, 7])
        cmpb = sb("cmpb", [H, 7, H], BF16)
        cnt = sb("cnt", [H, 7])
        acc = sb("acc", [H, 1])
        jnk = sb("jnk", [H, 7])
        eqx = sb("eqx", [H, H + 1])
        need = sb("need", [H, 1])
        bone = sb("bone", [H, H, 6], BF16)
        sp3 = sb("sp3", [H, 3, H], BF16)
        RHf = PG[:, :, 0:15].bitcast(BF16)
        RH = RHf.rearrange("p h (j b) -> p h j b", b=6)
        aoh = [sb(f"aoh{i}", [H, AR, 128], BF16) for i in range(2)]
        base = sb("base", [128, 1])
        lst = sb("lst", [128, 30])
        pix, stok, qtok, sd, rs, bh = [sb(n, [128, 6]) for n in ("pix", "stok", "qtok", "sd", "rs", "bh")]
        pixi = sb("pixi", [128, 6], U32)
        mv = sb("mv", [128, 6, 2])
        bs = sb("bs", [128, 6, 6])

        mx, mr = [sb(n, [128, 48]) for n in ("mx", "mr")]
        m3 = sb("m3", [128, 3, 48], BF16)
        m3T = sb("m3T", [48, 3, 128], BF16)
        rd = sb("rd", [128, 3, 4])
        X1 = sb("X1", [128, NCH, C])
        TK = sb("TK", [128, NCH, C])
        U = sb("U", [128, NCH, C])
        TT = sb("TT", [C, 2, HALF])
        V = sb("V", [128, NCH, NH, 32])
        OE = [sb(f"OE{i}", [128, HALF]) for i in range(2)]
        qmem = sb("qmem", [128, NH * KTOK // 2])
        kmem = sb("kmem", [128, NH * KTOK // 2])
        pmem = sb("pmem", [128, 4 * KTOK])
        QS = qmem[0:KROWS + 3, :].bitcast(BF16).rearrange("p (h n) -> p h n", h=NH)
        KS = kmem[0:KROWS + 3, :].bitcast(BF16).rearrange("p (h n) -> p h n", h=NH)
        HT = [qmem[:, 768 * i:768 * (i + 1)].rearrange("p (a n) -> p a n", a=2) for i in range(2)]
        LS = qmem[0:E, 1536:2304]
        lgs = [kmem[0:E, 8 * H * i:8 * H * (i + 1)] for i in range(2)]
        PR = [pmem[:, 768 * i:768 * (i + 1)].rearrange("p (a n) -> p a n", a=2) for i in range(4)]
        F = [U[:, :, :].rearrange("p c n -> p (c n)"), pmem[:, 0:768]]
        XG, XP = [pmem[:, 768 * i:768 * (i + 1)].rearrange("p (c n) -> p c n", c=NCH) for i in (0, 1)]
        QP, KP = [pmem[:, 768 + 1152 * i:1920 + 1152 * i].bitcast(BF16).rearrange("p (a n) -> p a n", a=3)
                  for i in range(2)]

        PD = [outer["psum"][i] for i in range(2)]
        PS = [outer["psum2"][i] for i in range(2)]
        PO = [outer["psum"][2 + i] for i in range(2)]

        def halves(ps):
            return ps[:, :, 0:HALF]

        def thirds(ps):
            return ps[:, :, 0:HALF].rearrange("p a (t c) -> p a t c", c=C)

        def six(t):
            return t[:, :, :].rearrange("p (a t) c -> p a t c", a=2)

        wloaded = sem("wloaded")
        wsummed = sem("wsummed")
        bn_root = sem("bn_root")
        pool_ready = sem("pool_ready")
        act_own, dve_own, pool_own = sem("act_own"), sem("dve_own"), sem("pool_own")
        x_in = [sem(f"x_in{i}") for i in range(2)]
        names = """setup_done rows_ready xt_copied pg_copied var_ready sd_ready maps_scaled conv_ready
            gelu_exp_ready cnt_ready totals_ready eq_ready eq_ranked sel_ready sel_ranked
            ranks_ready aoh_ready aoh_used y_factors y_rows y_rows_act y_stored var2_ready sd2_ready gate_factor
            chosen g_scaled lg_ready lg_staged lg_stored0 lg_stored1 rows_known tokens_in tokens_ready
            tt_ps tt_ready qkv_ps qk_copied qk_split heads_in v_ready max_ps max_read max_split maxT_ps
            maxT_ready max_in s_ps exp_done pv_done o_copied oT_ps o_ready wo_ps u_var sd3 h_ps h_ready
            ff_ps x1_ready tok_stored sel_lg_ps sel_lg_ready sel_lg_stored pool_half parts_out""".split()
        S = {n: sem(n) for n in names}

        def at(k, per, n):
            return k[0].times(per) + (k[1] * per + n)

        def number(k):
            return k[0].it + k[1]

        def rounds(eng, one):
            it = Round(eng, 0)
            one(it, (it, 0), None)
            with eng.Fori(1, B) as i:
                it = Round(eng, i)
                one(it, (it, 0), (it, -1))
            it = Round(eng, B)
            one(it, None, (it, -1))

        def tap_rows(i):
            d = DIL * i - PAD
            return d, max(0, -d), min(H, H - d)

        DENSE_A, DENSE_B = 3, 24
        MAX_DENSE = {3 * g + 2: DENSE_B + g for g in range(GROUPS - DENSE_B)}
        TAP_ORDER = [3, 0, 1, 2, 4, 5, 6]
        VAR_AT, SCALE_AT = 44, 46
        GELU_AT, SD2_AT = 2, 8
        SEARCH_AT = {10 + 3 * i: i for i in range(SEARCH)}
        EQ_AT, SEL_AT = 38, 44
        YACT_AT = range(10, 34)

        block = ctx.enter_context(nc.Block())

        @block.sync
        def _(sp):
            loads = [(K[:, :], io["const"]), (WG[:, 0:NTAP], io["conv_w"]), (WG[:, NTAP:MAPS], io["gateT"]), (Wqkv[:, :], io["wqkvT"]),
                     (Wo[:, :], io["woT"]), (W1[:, :], io["w1T"]),
                     (W2[:, :, :], io["w2T"].rearrange("(b p) c -> p b c", p=128))]
            for n, key in enumerate(("bv", "b_o", "ln1_g", "ln1_b", "b2", "ln2_g", "ln2_b")):
                loads.append((brow[:, n, :], io[key].partition_broadcast(128)))
            for n, key in enumerate(("bq", "bk", "b1a", "b1b")):
                loads.append((bcol[:, n:n + 1], io[key].rearrange("(p a) -> p a", a=1)))
            loads.append((bcol[0:E, 4:5], io["gate_b"].rearrange("(p a) -> p a", a=1)))
            for n, key in enumerate(("conv_b", "bn_g", "bn_b", "bn_m", "bn_v")):
                loads.append((bnp[:, n:n + 1], io[key].partition_broadcast(128)))
            assert len(loads) == NLOADS
            for dst, src in loads:
                sp.dma_start(dst, src).then_inc(wloaded, 16)


            def load(k, t):
                n = LAST_GROUP[t - 2] if t >= 2 else LAST_GROUP[t + NX - 2] - GROUPS
                sp.wait_ge(S["rows_ready"], at(k, GROUPS, GROUPS + n))
                m, row = CHUNK_ROWS[t], sum(CHUNK_ROWS[:t])
                sp.dma_start(XR[t % 2][:, 0:m * H],
                             io["x"][bass.ds(number(k), 1), :, row * H:(row + m) * H].rearrange("a c n -> (a c) n")
                             ).then_inc(x_in[t % 2], 16)

            def one(kd, ka, nxt):
                if kd is not None:
                    for t in range(2, NX):
                        load(kd, t)
                    for b in range(5):
                        if b < YD:
                            sp.wait_ge(S["y_rows"], at(kd, YD, b + 1))
                        else:
                            sp.wait_ge(S["y_rows_act"], at(kd, 5 - YD, b - YD + 1))
                        sp.dma_start(table[bass.ds(kd[0].times(ROWS) + b * BR * H, BR * H), :].rearrange("(h w) c -> w h c", w=H),
                                     XT[:, b * BR:(b + 1) * BR, :]).then_inc(S["y_stored"], 16)
                        sp.dma_start(scr["current"][b * BR * H:(b + 1) * BR * H, :].rearrange("(h w) c -> w h c", w=H),
                                     XT[:, b * BR:(b + 1) * BR, :]).then_inc(S["y_stored"], 16)
                if nxt is not None:
                    load(nxt, 0)
                    load(nxt, 1)
                if ka is not None:
                    sp.wait_ge(S["x1_ready"], at(ka, 1, 1))
                    sp.dma_start(table[bass.ds(ka[0].times(ROWS) + (NPIX - ROWS), KTOK), :].rearrange("(t p) c -> p t c", p=128),
                                 X1[:, :, :]).then_inc(S["tok_stored"], 16)
                    sp.wait_ge(S["sel_lg_ready"], at(ka, 1, 1))
                    sp.dma_start(logits[bass.ds(number(ka), 1), :, NPIX:ROWS].rearrange("a e n -> (a e) n"), LS
                                 ).then_inc(S["sel_lg_stored"], 16)

            it = Round(sp, 0)
            load((it, 0), 0)
            load((it, 0), 1)
            one((it, 0), None, (it, 1))
            with sp.Fori(1, B - 1) as i:
                it = Round(sp, i)
                one((it, 0), (it, -1), (it, 1))
            it = Round(sp, B - 1)
            one((it, 0), (it, -1), None)
            it = Round(sp, B)
            one(None, (it, -1), None)
            sp.wait_ge(S["y_stored"], B * 160)
            sp.wait_ge(S["tok_stored"], B * 16)
            sp.wait_ge(S["sel_lg_stored"], B * 16)

        @block.gpsimd
        def _(pool):
            def one(it, kd, ka):
                if ka is not None:
                    pool.wait_ge(S["qk_split"], at(ka, 1, 1))
                    for b in range(2):
                        pool.wait_ge(S[f"lg_stored{b}"], at(ka, 7 * 16, 7 * 16))
                    hold(pool, outer["pool_held"])
                    for n, parts in enumerate((QP, KP)):
                        pool.dma_start(scr["parts"][n, :, :, :], parts).then_inc(S["parts_out"], 16)
                    pool.wait_ge(S["parts_out"], at(ka, 32, 32))
                    hold(pool, outer["pool_held"])
                    for g, (pq, pk) in enumerate(((0, 0), (0, 1), (1, 0), (1, 1), (0, 2), (2, 0))):
                        for n, (dst, part) in enumerate(((QS, pq), (KS, pk))):
                            pool.dma_start(dst[g * HD:(g + 1) * HD, :, :],
                                           scr["parts"][n, :, part, :].rearrange("(h d) n -> d h n", d=HD)
                                           ).then_inc(S["heads_in"], 16)
                    pool.wait_ge(S["maxT_ready"], at(ka, 1, 1))
                    hold(pool, outer["pool_held"])
                    for j in range(3):
                        pool.dma_start(QS[KROWS + j:KROWS + j + 1, :, :].rearrange("p h (q n) -> p (h q) n", n=128),
                                       m3T[:, j, :]).then_inc(S["max_in"], 16)
                if kd is not None:
                    pool.wait_ge(S["gate_factor"], at(kd, 1, 1))
                    for b in range(5):
                        rows = slice(b * BR, (b + 1) * BR)
                        nc.gpsimd.tensor_tensor(PG[:, rows, NTAP:MAPS], PG[:, rows, NTAP:MAPS],
                                                bc(gsc[:, rows], [H, BR, E], 2), ALU.mult).then_inc(S["pool_half"], 1)
                    pool.wait_ge(S["chosen"], at(kd, 1, 1))
                    pool.wait_ge(S["pool_half"], at(kd, 5, 5))
                    for b in range(5):
                        rows = slice(b * BR, (b + 1) * BR)
                        nc.gpsimd.tensor_tensor(PG[:, rows, NTAP:MAPS], PG[:, rows, NTAP:MAPS],
                                                bc(neg[:, rows], [H, BR, E], 2), ALU.add).then_inc(S["g_scaled"], 1)
                    pool.wait_ge(S["rows_known"], at(kd, 1, 1))
                    pool.wait_ge(S["y_stored"], at(kd, 160, 160))
                    if ka is not None:
                        pool.wait_ge(S["pv_done"], at(ka, 24, 24))
                    hold(pool, outer["pool_held"])
                    for c in range(NCH):
                        pool.indirect_dma_start(XG[:, c, :], None, scr["current"][:, :],
                                                bass.IndirectOffsetOnAxis(ap=pixi[:, c:c + 1], axis=0)
                                                ).then_inc(S["tokens_in"], 16)
                        pool.indirect_dma_start(XP[:, c, :], None, io["pos"][:, :],
                                                bass.IndirectOffsetOnAxis(ap=pixi[:, c:c + 1], axis=0)
                                                ).then_inc(S["tokens_in"], 16)
                if ka is not None:
                    pool.wait_ge(S["sel_lg_stored"], at(ka, 16, 16))
                    hold(pool, outer["pool_held"])

            rounds(pool, one)

        @block.scalar
        def _(act):
            a_ = nc.scalar
            act.wait_ge(wloaded, NLOADS * 16)
            act.wait_ge(pool_ready, 1)
            a_.activation(bna[:, 0:1], bnp[:, 4:5], ACT.Sqrt, bias=eps[:, 1:2]).then_inc(bn_root, 1)

            def one(it, kd, ka):
                own = Own(act, act_own, it, ACT_PER)

                def dense(g):
                    n = min(4, H - 4 * g)
                    act.wait_ge(S["rows_ready"], at(kd, GROUPS, GROUPS + g + 1))
                    a_.activation(XT[:, 4 * g:4 * g + n, :], PD[g % 2][0:H, 0:n * C].rearrange("p (a c) -> p a c", a=n),
                                  ACT.Copy).then_inc(S["xt_copied"], 1)
                    a_.activation(PG[:, 4 * g:4 * g + n, :], PO[g % 2][0:H, 0:n * MAPS].rearrange("p (a m) -> p a m", a=n),
                                  ACT.Copy).then_inc(S["pg_copied"], 1)

                def turned(ps, n):
                    act.wait_ge(S["tt_ps"], at(ka, 4, n))
                    a_.activation(TT[:, :, :], halves(ps), ACT.Copy).then_inc(S["tt_ready"], 1)

                def root(n):
                    act.wait_ge(S["u_var"], at(ka, 3, n))
                    a_.activation(sd[:, :], mv[:, :, 1], ACT.Sqrt, bias=eps[:, 1:2]).then_inc(S["sd3"], 1)

                def gate_logits(first, last):
                    for q in range(first, last):
                        n = min(4, H - 4 * q)
                        b = q // 2
                        act.wait_ge(S["lg_ready"], at(kd, LG, q + 1))
                        if q % 2 == 0 and b >= 2:
                            act.wait_ge(S[f"lg_stored{b % 2}"], at(kd, 7 * 16, 16 * (b // 2)))
                        ins = a_.activation(lgs[b % 2][:, (q % 2) * 4 * H:(q % 2) * 4 * H + n * H],
                                            PO[q % 2][0:E, 0:n * H], ACT.Identity, bias=bcol[0:E, 4:5])
                        ins.then_inc(S["lg_staged"], 1)
                        if q % 2:
                            rows = 8 if b < 13 else 6
                            act.wait_ge(S["lg_staged"], at(kd, LG, q + 1))
                            act.dma_start(logits[bass.ds(number(kd), 1), :, b * 8 * H:b * 8 * H + rows * H].rearrange(
                                "a e n -> (a e) n"), lgs[b % 2][:, 0:rows * H]).then_inc(S[f"lg_stored{b % 2}"], 16)

                def spread_rows(first, last):
                    for h in range(first, last):
                        ins = a_.activation(XT[:, h, :], XT[:, h, :], ACT.Identity, bias=Bn[:, h:h + 1], scale=A1[:, h:h + 1])
                        if h % BR == BR - 1:
                            ins.then_inc(S["y_rows_act"], 1)

                if kd is not None:
                    if ka is not None:
                        act.wait_ge(S["y_stored"], at(ka, 160, 160))
                    for g in range(DENSE_A):
                        dense(g)
                if ka is not None:
                    turned(PS[0], 1)
                    act.wait_ge(S["qkv_ps"], at(ka, 3, 1))
                    a_.activation(F[0].rearrange("p (a n) -> p a n", a=2), halves(PS[1]), ACT.Identity, bias=bna[:, 3:4],
                                  scale=0.25).then_inc(S["qk_copied"], 1)
                    act.wait_ge(S["qkv_ps"], at(ka, 3, 2))
                    a_.activation(F[1].rearrange("p (a n) -> p a n", a=2), halves(PS[0]), ACT.Identity, bias=bcol[:, 1:2]
                                  ).then_inc(S["qk_copied"], 1)
                if kd is not None:
                    for g in range(DENSE_A, GROUPS):
                        dense(g)
                    act.wait_ge(S["var_ready"], at(kd, 1, 1))
                    a_.activation(t1[:, :], var[:, :], ACT.Sqrt, bias=eps[0:H, 0:1]).then_inc(S["sd_ready"], 1)
                rows_left = list(range(YD * BR, H))
                for n in range(48):
                    if kd is not None and n == GELU_AT:
                        act.wait_ge(S["conv_ready"], at(kd, 1, 1))
                        own.link(a_.activation(t0[:, :], PO[0][0:H, 0:H], ACT.Gelu, bias=bna[0:H, 2:3], scale=bna[0:H, 1:2]))
                        a_.activation(imp[:, :], t0[:, :], ACT.Exp, scale=-1.0).then_inc(S["gelu_exp_ready"], 1)
                    if kd is not None and n == SD2_AT:
                        act.wait_ge(S["var2_ready"], at(kd, 1, 1))
                        a_.activation(t0[:, :], gsc[:, :], ACT.Sqrt, bias=eps[0:H, 1:2]).then_inc(S["sd2_ready"], 1)
                    if kd is not None and n in YACT_AT:
                        first = YD * BR + (n - YACT_AT[0]) * (H - YD * BR) // len(YACT_AT)
                        last = YD * BR + (n + 1 - YACT_AT[0]) * (H - YD * BR) // len(YACT_AT)
                        spread_rows(first, last)
                    if ka is None:
                        continue
                    act.wait_ge(S["s_ps"], at(ka, 48, n + 1))
                    if n >= 4:
                        act.wait_ge(S["pv_done"], at(ka, 24, n // 2 - 1))
                    a_.activation(PR[n % 4][:, :, :], halves(PS[n % 2]), ACT.Exp).then_inc(S["exp_done"], 1)
                    if n % 12 == 3 and n > 12:
                        heads_out(act, ka, n // 12 - 1)
                if ka is not None:
                    heads_out(act, ka, 3)
                    turned(PS[1], 2)
                    root(1)
                if kd is not None:
                    gate_logits(0, 10)
                if ka is not None:
                    turned(PS[1], 3)
                    for b in range(2):
                        act.wait_ge(S["h_ps"], at(ka, 2, b + 1))
                        a_.activation(HT[b][:, :, :], halves(PS[b]), ACT.Relu, bias=bcol[:, 2 + b:3 + b]
                                      ).then_inc(S["h_ready"], 1)
                if kd is not None:
                    gate_logits(10, 16)
                if ka is not None:
                    root(2)
                if kd is not None:
                    gate_logits(16, LG)
                if ka is not None:
                    root(3)
                    turned(PS[1], 4)
                    act.wait_ge(S["sel_lg_ps"], at(ka, 1, 1))
                    a_.activation(LS.rearrange("p (a n) -> p a n", a=2), halves(PS[0])[0:E], ACT.Identity,
                                  bias=bcol[0:E, 4:5]).then_inc(S["sel_lg_ready"], 1)
                own.pad()

            def heads_out(act, ka, g):
                act.wait_ge(S["pv_done"], at(ka, 24, 6 * g + 6))
                if g >= 2:
                    act.wait_ge(S["oT_ps"], at(ka, 4, g - 1))
                a_.activation(OE[g % 2][:, :], PD[g % 2][:, 0:HALF], ACT.Copy).then_inc(S["o_copied"], 1)

            rounds(act, one)
            for b in range(2):
                act.wait_ge(S[f"lg_stored{b}"], B * 7 * 16)

        @block.vector
        def _(dve):
            v = nc.vector
            once = Own(dve, dve_own, 0, 0)
            once.step(v.memset(eps[:, 0:1], 1e-6))
            once.step(v.memset(eps[:, 1:2], 1e-5))
            once.step(v.memset(base[:, :], 0.0))
            once.step(v.memset(V[:, :, :, :], 0.0))
            once.step(v.memset(KS[KROWS:KROWS + 3, :, :], 1.0))
            dve.wait_ge(wloaded, NLOADS * 16)
            once.link(v.tensor_copy(identb[:, :], ident))
            once.link(v.memset(V[:, :, :, HD:HD + 1], 1.0))
            dve.sem_inc(pool_ready, 1)
            dve.wait_ge(wsummed, 1)
            once.link(v.scalar_tensor_tensor(WGc[:, :], PO[0][:, 0:MAPS], -1.0 / C, WG[:, :], ALU.mult, ALU.add))
            dve.wait_ge(bn_root, 1)
            once.link(v.reciprocal(bna[:, 1:2], bna[:, 0:1]))
            once.link(v.tensor_tensor(bna[:, 1:2], bna[:, 1:2], bnp[:, 1:2], ALU.mult))
            once.link(v.tensor_tensor(bna[:, 2:3], bnp[:, 0:1], bnp[:, 3:4], ALU.subtract))
            once.link(v.tensor_tensor(bna[:, 2:3], bna[:, 2:3], bna[:, 1:2], ALU.mult))
            once.link(v.tensor_tensor(bna[:, 2:3], bna[:, 2:3], bnp[:, 2:3], ALU.add))
            once.link(v.tensor_scalar(bna[:, 3:4], bcol[:, 0:1], 0.25, None, ALU.mult))
            once.per = DVE_PER
            once.pad()
            dve.sem_inc(S["setup_done"], 1)

            def one(it, kd, ka):
                own = Own(dve, dve_own, it, DVE_PER, before=DVE_PER)
                link, step = own.link, own.step

                def dense(g):
                    n = min(4, H - 4 * g)
                    dve.wait_ge(S["xt_copied"], at(kd, GROUPS, g + 1))
                    for h in range(4 * g, 4 * g + n):
                        step(v.bn_stats(ST[:, h, :], XT[:, h, :]))

                def stats(src):
                    for c in range(NCH):
                        step(v.bn_stats(bs[:, c, :], src[:, c, :]))
                    own.wait()
                    combine(v, own, mv, bs, bh)

                def rank():
                    step(v.tensor_copy(t0[:, :], PO[0][0:H, 0:H]))
                    link(v.tensor_copy(t1[:, :], PO[1][0:H, 0:H]))
                    link(v.tensor_tensor_scan(ar[:, :], K[0:H, C_ONE:C_ONE + H], t0[:, :], 0.0, ALU.mult, ALU.add))
                    link(v.tensor_tensor(ar[:, :], ar[:, :], t0[:, :], ALU.subtract))
                    link(v.tensor_tensor(ar[:, :], ar[:, :], t1[:, :], ALU.add))

                def tokens():
                    link(v.tensor_scalar(rs[:, :], stok[:, :], 1.0, None, ALU.add))
                    link(v.reciprocal(rs[:, :], rs[:, :]))
                    link(v.tensor_tensor(qtok[:, :], rs[:, :], stok[:, :], ALU.mult))
                    dve.wait_ge(S["tokens_in"], at(ka, 192, 192))
                    stats(XG)
                    for c in range(NCH):
                        step(v.tensor_scalar(TK[:, c, :], XG[:, c, :], mv[:, c, 0:1], qtok[:, c:c + 1],
                                             ALU.subtract, ALU.mult))
                    own.wait()
                    link(v.tensor_tensor(X1[:, :, :], XG[:, :, :], TK[:, :, :], ALU.subtract))
                    v.tensor_tensor(TK[:, :, :], TK[:, :, :], XP[:, :, :], ALU.add).then_inc(S["tokens_ready"], 1)
                    for n, parts in ((0, QP), (1, KP)):
                        dve.wait_ge(S["qk_copied"], at(ka, 2, n + 1))
                        for p in range(2):
                            link(v.tensor_copy(parts[:, p, :], F[n]))
                            link(v.tensor_tensor(F[n], F[n], parts[:, p, :], ALU.subtract))
                        link(v.tensor_copy(parts[:, 2, :], F[n]))
                    dve.sem_inc(S["qk_split"], 1)
                    dve.wait_ge(S["qkv_ps"], at(ka, 3, 3))
                    v.tensor_tensor(V[:, :, :, 0:HD].rearrange("p (a t) h d -> p a t h d", a=2),
                                    thirds(PS[1]).rearrange("p a t (h d) -> p a t h d", d=HD),
                                    bc(bc(brow[:, 0, :], [128, 3, C], 1), [128, 2, 3, C], 1).rearrange(
                                        "p a t (h d) -> p a t h d", d=HD), ALU.add).then_inc(S["v_ready"], 1)

                def heads_out(g):
                    dve.wait_ge(S["oT_ps"], at(ka, 4, g + 1))
                    hg, half = g // 2, g % 2
                    pv = PD[g % 2][:, 0:HALF].rearrange("p (t j d) -> p t j d", t=3, d=32)
                    if g:
                        dve.wait_ge(S["o_ready"], at(ka, 4, g))
                    link(v.reciprocal(rd[:, :, :], pv[:, :, :, HD]))
                    v.tensor_tensor(U[:, 3 * half:3 * half + 3, 64 * hg:64 * hg + 64].rearrange("p t (j d) -> p t j d", d=HD),
                                    pv[:, :, :, 0:HD], bc(rd[:, :, :], [128, 3, 4, HD], 3), ALU.mult
                                    ).then_inc(S["o_ready"], 1)

                def variance():
                    own.wait()
                    step(v.tensor_tensor(mean[:, :], ST[:, :, 1], ST[:, :, 4], ALU.add))
                    step(v.tensor_tensor(t0[:, :], ST[:, :, 1], ST[:, :, 4], ALU.subtract))
                    link(v.tensor_tensor(var[:, :], ST[:, :, 2], ST[:, :, 5], ALU.add))
                    step(v.tensor_scalar(mean[:, :], mean[:, :], 0.5, None, ALU.mult))
                    step(v.tensor_scalar(var[:, :], var[:, :], 1.0 / C, None, ALU.mult))
                    link(v.tensor_scalar(t0[:, :], t0[:, :], 0.5, None, ALU.mult))
                    link(v.tensor_tensor(t0[:, :], t0[:, :], t0[:, :], ALU.mult))
                    v.tensor_tensor(var[:, :], var[:, :], t0[:, :], ALU.add).then_inc(S["var_ready"], 1)

                def scale_maps():
                    dve.wait_ge(S["sd_ready"], at(kd, 1, 1))
                    link(v.reciprocal(r[:, :], t1[:, :]))
                    dve.wait_ge(S["pg_copied"], at(kd, GROUPS, GROUPS))
                    v.tensor_tensor(PG[:, :, 0:NTAP], PG[:, :, 0:NTAP], bc(r[:, :], [H, H, NTAP], 2), ALU.mult
                                    ).then_inc(S["maps_scaled"], 1)

                def importance():
                    dve.wait_ge(S["gelu_exp_ready"], at(kd, 1, 1))
                    link(v.tensor_scalar(imp[:, :], imp[:, :], 1.0, None, ALU.add))
                    link(v.reciprocal(imp[:, :], imp[:, :]))
                    link(v.tensor_tensor(s[:, :], r[:, :], imp[:, :], ALU.mult))
                    step(v.tensor_scalar(A1[:, :], s[:, :], 1.0, None, ALU.add))
                    link(v.scalar_tensor_tensor(Bn[:, :], mean[:, :], -1.0, s[:, :], ALU.mult, ALU.mult))
                    link(v.tensor_tensor(t1[:, :], A1[:, :], A1[:, :], ALU.mult))
                    v.tensor_tensor(gsc[:, :], t1[:, :], var[:, :], ALU.mult).then_inc(S["var2_ready"], 1)

                def gate_factor():
                    dve.wait_ge(S["sd2_ready"], at(kd, 1, 1))
                    link(v.reciprocal(t1[:, :], t0[:, :]))
                    v.tensor_tensor(gsc[:, :], A1[:, :], t1[:, :], ALU.mult).then_inc(S["gate_factor"], 1)

                def spread_rows(first, last):
                    for h in range(first, last):
                        ins = v.tensor_scalar(XT[:, h, :], XT[:, h, :], A1[:, h:h + 1], Bn[:, h:h + 1], ALU.mult, ALU.add)
                        if h % BR == BR - 1:
                            ins.then_inc(S["y_rows"], 1)

                def search(i):
                    if i == 0:
                        link(v.memset(thr[:, :], 0.25))
                    m = 7 if i < SEARCH - 1 else 1
                    u = 8.0 ** -(i + 1) if i < SEARCH - 1 else 2.0 ** -25
                    link(v.tensor_scalar(ths[:, 0:m], K[0:H, C_TH:C_TH + m], u, thr[:, 0:1], ALU.mult, ALU.add))
                    link(v.tensor_tensor(cmpb[:, 0:m, :], bc(imp[:, :], [H, m, H], 1), bc(ths[:, 0:m], [H, m, H], 2),
                                         ALU.is_ge))
                    v.tensor_reduce(cnt[:, 0:m], cmpb[:, 0:m, :], AX.X, ALU.add).then_inc(S["cnt_ready"], 1)
                    spread_rows(i * YD * BR // SEARCH, (i + 1) * YD * BR // SEARCH)
                    dve.wait_ge(S["totals_ready"], at(kd, SEARCH, i + 1))
                    link(v.tensor_scalar(jnk[:, 0:m], PO[1][0:H, 0:m], KTOK - 0.5, None, ALU.is_ge))
                    link(v.tensor_reduce(acc[:, :], jnk[:, 0:m], AX.X, ALU.add))
                    link(v.scalar_tensor_tensor(thr[:, :], acc[:, :], u, thr[:, :], ALU.mult, ALU.add))

                def masks():
                    step(v.tensor_scalar(eqx[:, 0:H], imp[:, :], thr[:, 0:1], None, ALU.is_equal))
                    link(v.tensor_scalar(gt[:, :], imp[:, :], thr[:, 0:1], None, ALU.is_gt))
                    v.tensor_reduce(eqx[:, H:H + 1], gt[:, :], AX.X, ALU.add).then_inc(S["eq_ready"], 1)

                def choose():
                    dve.wait_ge(S["eq_ranked"], at(kd, 1, 1))
                    step(v.tensor_scalar(need[:, :], PO[0][0:H, H:H + 1], -1.0, float(KTOK), ALU.mult, ALU.add))
                    rank()
                    link(v.tensor_scalar(ar[:, :], ar[:, :], need[:, :], None, ALU.is_lt))
                    link(v.tensor_tensor(ar[:, :], ar[:, :], eqx[:, 0:H], ALU.mult))
                    v.tensor_tensor(sel[:, :], ar[:, :], gt[:, :], ALU.add).then_inc(S["sel_ready"], 1)
                    dve.wait_ge(S["sel_ready"], at(kd, 1, 1))
                    v.tensor_scalar(neg[:, :], sel[:, :], NEG, None, ALU.mult).then_inc(S["chosen"], 1)

                def list_operands():
                    dve.wait_ge(S["sel_ranked"], at(kd, 1, 1))
                    rank()
                    link(v.tensor_scalar(t0[:, :], sel[:, :], -4096.0, 4096.0, ALU.mult, ALU.add))
                    link(v.tensor_tensor(ar[:, :], ar[:, :], t0[:, :], ALU.add))
                    link(v.tensor_tensor(cmpb[:, :, :], bc(ar[:, :], [H, 7, H], 1),
                                         bc(K[0:H, C_RAMP:C_RAMP + 7], [H, 7, H], 2), ALU.is_ge))
                    step(v.tensor_tensor(bone[:, :, :].rearrange("p h b -> p b h"), cmpb[:, 0:6, :], cmpb[:, 1:7, :],
                                         ALU.subtract))
                    step(v.tensor_reduce(t0[:, :], cmpb[:, 1:6, :].rearrange("p m h -> p h m"), AX.X, ALU.add))
                    link(v.tensor_copy(sp3[:, 0, :], s[:, :]))
                    step(v.tensor_tensor(t1[:, :], s[:, :], sp3[:, 0, :], ALU.subtract))
                    link(v.scalar_tensor_tensor(ar[:, :], t0[:, :], -128.0, ar[:, :], ALU.mult, ALU.add))
                    link(v.tensor_copy(sp3[:, 1, :], t1[:, :]))
                    link(v.tensor_tensor(sp3[:, 2, :], t1[:, :], sp3[:, 1, :], ALU.subtract))
                    step(v.tensor_scalar(RH[:, :, 0, :], bone[:, :, :], K[0:H, C_W:C_W + 1], None, ALU.mult))
                    step(v.tensor_tensor(RH[:, :, 1, :], bone[:, :, :], bc(K[0:H, C_HROW:C_HROW + H], [H, H, 6], 2),
                                         ALU.mult))
                    for j in range(3):
                        step(v.tensor_tensor(RH[:, :, 2 + j, :], bone[:, :, :], bc(sp3[:, j, :], [H, H, 6], 2), ALU.mult))
                    own.wait()
                    dve.sem_inc(S["ranks_ready"], 1)

                def one_hots():
                    for b in range(NA):
                        if b >= 2:
                            dve.wait_ge(S["aoh_used"], at(kd, NA, b - 1))
                        v.tensor_tensor(aoh[b % 2][:, :, :], bc(K[0:H, C_IOTA:C_IOTA + 128], [H, AR, 128], 1),
                                        bc(ar[:, b * AR:(b + 1) * AR], [H, AR, 128], 2), ALU.is_equal
                                        ).then_inc(S["aoh_ready"], 1)

                def read_list():
                    dve.wait_ge(S["aoh_used"], at(kd, NA, NA))
                    link(v.tensor_copy(lst[:, :], PD[0][:, 0:30]))
                    step(v.tensor_tensor(stok[:, :], lst[:, 12:18], lst[:, 18:24], ALU.add))
                    link(v.scalar_tensor_tensor(pix[:, :], lst[:, 6:12], float(H), lst[:, 0:6], ALU.mult, ALU.add))
                    step(v.tensor_copy(pixi[:, :], pix[:, :]))
                    step(v.tensor_scalar(pix[:, :], pix[:, :], base[:, 0:1], None, ALU.add))
                    link(v.tensor_tensor(stok[:, :], stok[:, :], lst[:, 24:30], ALU.add))
                    step(v.tensor_scalar(base[:, :], base[:, :], float(ROWS), None, ALU.add))
                    v.tensor_copy(lists[:, bass.ds(kd[0].times(6), 6)], pix[:, :]).then_inc(S["rows_known"], 1)

                def norm_stats(n):
                    stats(U)
                    dve.sem_inc(S["u_var"], 1)

                def norm(gi, n):
                    dve.wait_ge(S["sd3"], at(ka, 3, n))
                    link(v.reciprocal(rs[:, :], sd[:, :]))
                    for c in range(NCH):
                        step(v.tensor_scalar(U[:, c, :], U[:, c, :], mv[:, c, 0:1], rs[:, c:c + 1], ALU.subtract, ALU.mult))
                    own.wait()
                    if gi is not None:
                        link(v.tensor_tensor(U[:, :, :], U[:, :, :], bc(brow[:, gi, :], [128, NCH, C], 1), ALU.mult))

                def residual(ready, row):
                    dve.wait_ge(S[ready], at(ka, 1, 1))
                    link(v.tensor_tensor(six(U), thirds(PS[0]), six(TK), ALU.add))
                    link(v.tensor_tensor(U[:, :, :], U[:, :, :], bc(brow[:, row, :], [128, NCH, C], 1), ALU.add))

                D, A = kd is not None, ka is not None
                if D:
                    for g in range(DENSE_A):
                        dense(g)
                if A:
                    tokens()
                if D:
                    for g in range(DENSE_A, DENSE_B):
                        dense(g)
                for n in range(48):
                    if A:
                        dve.wait_ge(S["max_ps"], at(ka, 48, n + 1))
                        v.tensor_reduce(mx[:, n:n + 1], halves(PS[n % 2]), AX.XY, ALU.max).then_inc(S["max_read"], 1)
                    if D and n in MAX_DENSE:
                        dense(MAX_DENSE[n])
                    if D and n == VAR_AT:
                        variance()
                    if D and n == SCALE_AT:
                        scale_maps()
                if A:
                    dve.wait_ge(S["max_read"], at(ka, 48, 48))
                    link(v.tensor_scalar(mx[:, :], mx[:, :], -1.0, None, ALU.mult))
                    link(v.tensor_copy(m3[:, 0, :], mx[:, :]))
                    link(v.tensor_tensor(mr[:, :], mx[:, :], m3[:, 0, :], ALU.subtract))
                    link(v.tensor_copy(m3[:, 1, :], mr[:, :]))
                    v.tensor_tensor(m3[:, 2, :], mr[:, :], m3[:, 1, :], ALU.subtract).then_inc(S["max_split"], 1)
                    dve.wait_ge(S["maxT_ps"], at(ka, 1, 1))
                    v.tensor_copy(m3T[:, :, :], PO[1][0:48, :].bitcast(BF16)[:, 0:384].rearrange("p (a n) -> p a n", a=3)
                                  ).then_inc(S["maxT_ready"], 1)
                if D:
                    importance()
                    gate_factor()
                for i in range(SEARCH):
                    if A and i == 3:
                        heads_out(0)
                    if A and i == 7:
                        heads_out(1)
                    if D:
                        search(i)
                if D:
                    masks()
                    choose()
                if A:
                    heads_out(2)
                if D:
                    list_operands()
                if A:
                    heads_out(3)
                if A:
                    residual("wo_ps", 1)
                    norm_stats(1)
                    norm(2, 1)
                    v.tensor_tensor(TK[:, :, :], U[:, :, :], bc(brow[:, 3, :], [128, NCH, C], 1), ALU.add
                                    ).then_inc(S["tokens_ready"], 1)
                if D:
                    one_hots()
                if A:
                    dve.wait_ge(S["tokens_ready"], at(ka, 3, 2))
                    residual("ff_ps", 4)
                    norm_stats(2)
                if D:
                    read_list()
                if A:
                    norm(5, 2)
                    link(v.tensor_tensor(U[:, :, :], U[:, :, :], bc(brow[:, 6, :], [128, NCH, C], 1), ALU.add))
                    link(v.tensor_tensor(U[:, :, :], U[:, :, :], X1[:, :, :], ALU.add))
                    v.tensor_copy(X1[:, :, :], U[:, :, :]).then_inc(S["x1_ready"], 1)
                    norm_stats(3)
                    norm(None, 3)
                    dve.sem_inc(S["tokens_ready"], 1)
                    dve.wait_ge(S["tok_stored"], at(ka, 16, 16))
                own.pad()

            rounds(dve, one)

        @block.tensor
        def _(pe):
            t = nc.tensor
            pe.sem_inc(S["rows_ready"], GROUPS)
            pe.wait_ge(wloaded, NLOADS * 16)
            t.matmul(PO[0][:, 0:MAPS], K[:, C_ONE:C_ONE + 128], WG[:, :], start=True, stop=True).then_inc(wsummed, 1)
            pe.wait_ge(S["setup_done"], 1)

            def one(it, kd, ka):
                D, A = kd is not None, ka is not None

                def dense(g):
                    c = g // 2
                    if g % 2 == 0:
                        pe.wait_ge(x_in[c % 2], at(kd, NX // 2 * 16, 16 * (c // 2 + 1)))
                    if g >= 2:
                        pe.wait_ge(S["xt_copied"], at(kd, GROUPS, g - 1))
                        pe.wait_ge(S["pg_copied"], at(kd, GROUPS, g - 1))
                    for j in range(min(4, H - 4 * g)):
                        at_row = (g % 2) * 4 + j
                        xs = XR[c % 2][:, at_row * H:(at_row + 1) * H]
                        t.transpose(PD[g % 2][0:H, j * C:(j + 1) * C], xs, ident)
                        ins = t.matmul(PO[g % 2][0:H, j * MAPS:(j + 1) * MAPS], xs, WGc[:, :], start=True, stop=True)
                    ins.then_inc(S["rows_ready"], 1)

                def conv(i):
                    d, lo, hi = tap_rows(i)
                    if i == TAP_ORDER[0]:
                        pe.wait_ge(S["maps_scaled"], at(kd, 1, 1))
                    for j in range(TAPS):
                        ins = t.matmul(PO[0][0:H, lo:hi], K[0:H, C_SH + j * H:C_SH + (j + 1) * H],
                                       PG[:, lo + d:hi + d, i * TAPS + j], start=(i == TAP_ORDER[0] and j == 0),
                                       stop=(i == TAP_ORDER[-1] and j == TAPS - 1))
                    if i == TAP_ORDER[-1]:
                        ins.then_inc(S["conv_ready"], 1)

                def totals(i):
                    m = 7 if i < SEARCH - 1 else 1
                    pe.wait_ge(S["cnt_ready"], at(kd, SEARCH, i + 1))
                    t.matmul(PO[1][0:H, 0:m], onesH, cnt[:, 0:m], start=True, stop=True).then_inc(S["totals_ready"], 1)

                def ranks(ready, mask, n, ranked):
                    pe.wait_ge(S[ready], at(kd, 1, 1))
                    t.matmul(PO[0][0:H, 0:n], onesH, mask[:, 0:n], start=True, stop=True)
                    t.matmul(PO[1][0:H, 0:H], K[0:H, C_LT:C_LT + H], mask[:, 0:H], start=True, stop=True
                             ).then_inc(S[ranked], 1)

                def the_list():
                    for b in range(NA):
                        pe.wait_ge(S["aoh_ready"], at(kd, NA, b + 1))
                        for i in range(AR):
                            h = b * AR + i
                            ins = t.matmul(PD[0][:, 0:30], aoh[b % 2][:, i, :], RHf[:, h, :], start=(h == 0), stop=(h == H - 1))
                        ins.then_inc(S["aoh_used"], 1)

                def gate_logits(first, last):
                    for q in range(first, last):
                        n = min(4, H - 4 * q)
                        pe.wait_ge(S["g_scaled"], at(kd, 5, (4 * q + n - 1) // BR + 1))
                        if q == 0:
                            pe.wait_ge(S["ranks_ready"], at(kd, 1, 1))
                        if q >= 2:
                            pe.wait_ge(S["lg_staged"], at(kd, LG, q - 1))
                        hold(pe, outer["pe_held"])
                        for i in range(n):
                            ins = t.transpose(PO[q % 2][0:E, i * H:(i + 1) * H], PG[:, 4 * q + i, NTAP:MAPS], identH)
                        ins.then_inc(S["lg_ready"], 1)

                def turn(src, ps):
                    for c in range(NCH):
                        ins = t.transpose(ps[:, c // 3, (c % 3) * 128:(c % 3) * 128 + 128], src[:, c, :], ident)
                    ins.then_inc(S["tt_ps"], 1)

                def project(ps, w, inc):
                    for a in range(2):
                        ins = t.matmul(ps[0:w.shape[1], a, 0:HALF], w, TT[:, a, :], start=True, stop=True)
                    ins.then_inc(inc, 1)

                def project_rows(ps, w, inc):
                    for c in range(NCH):
                        ins = t.matmul(ps[:, c // 3, (c % 3) * 128:(c % 3) * 128 + 128],
                                       TT[:, c // 3, (c % 3) * 128:(c % 3) * 128 + 128], w, start=True, stop=True)
                    ins.then_inc(inc, 1)

                def weigh(m):
                    g, kc = m // 6, m % 6
                    pe.wait_ge(S["exp_done"], at(ka, 48, 2 * m + 2))
                    if kc == 0 and g >= 2:
                        pe.wait_ge(S["o_ready"], at(ka, 4, g - 1))
                    for j in range(4):
                        ins = t.matmul(PD[g % 2][32 * j:32 * j + 32, 0:HALF], V[:, kc, 4 * (g // 2) + j, :],
                                       PR[(2 * m + j // 2) % 4][:, j % 2, :], start=(kc == 0), stop=(kc == NCH - 1))
                    ins.then_inc(S["pv_done"], 1)

                def turn_heads(g):
                    pe.wait_ge(S["o_copied"], at(ka, 4, g + 1))
                    for c in range(3):
                        ins = t.transpose(PD[g % 2][:, c * 128:(c + 1) * 128], OE[g % 2][:, c * 128:(c + 1) * 128], ident)
                    ins.then_inc(S["oT_ps"], 1)

                if D:
                    for g in range(DENSE_A):
                        dense(g)
                if A:
                    pe.wait_ge(S["tokens_ready"], at(ka, 3, 1))
                    turn(TK, PS[0])
                    pe.wait_ge(S["tt_ready"], at(ka, 4, 1))
                    project(PS[1], Wqkv[:, 0:C], S["qkv_ps"])
                    project(PS[0], Wqkv[:, C:2 * C], S["qkv_ps"])
                    pe.wait_ge(S["qk_copied"], at(ka, 2, 1))
                    project_rows(PS[1], Wqkv[:, 2 * C:3 * C], S["qkv_ps"])
                if D:
                    for g in range(DENSE_A, DENSE_B):
                        dense(g)
                if A:
                    pe.wait_ge(S["heads_in"], at(ka, 2 * SLOTS * 16, 2 * SLOTS * 16))
                    pe.wait_ge(S["qk_copied"], at(ka, 2, 2))
                    pe.wait_ge(S["v_ready"], at(ka, 1, 1))
                for n in range(48):
                    if A:
                        h, q = n // 6, n % 6
                        if n >= 2:
                            pe.wait_ge(S["max_read"], at(ka, 48, n - 1))
                        for a in range(2):
                            ins = t.matmul(PS[n % 2][:, a, 0:HALF], QS[0:KROWS, h, q * 128:(q + 1) * 128],
                                           KS[0:KROWS, h, a * HALF:(a + 1) * HALF], start=True, stop=True)
                        ins.then_inc(S["max_ps"], 1)
                    if D and n in MAX_DENSE:
                        dense(MAX_DENSE[n])
                if A:
                    pe.wait_ge(S["max_split"], at(ka, 1, 1))
                    if D:
                        pe.wait_ge(S["pg_copied"], at(kd, GROUPS, GROUPS))
                        pe.wait_ge(S["xt_copied"], at(kd, GROUPS, GROUPS))
                    hold(pe, outer["pe_held"])
                    for j in range(3):
                        ins = t.transpose(PO[1][0:48, :].bitcast(BF16)[:, 128 * j:128 * j + 128], m3[:, j, :], identb[:, :])
                    ins.then_inc(S["maxT_ps"], 1)
                if D:
                    for i in TAP_ORDER:
                        conv(i)
                if A:
                    pe.wait_ge(S["max_in"], at(ka, 48, 48))
                for n in range(48):
                    if D and n in SEARCH_AT:
                        totals(SEARCH_AT[n])
                    if D and n == EQ_AT:
                        ranks("eq_ready", eqx, H + 1, "eq_ranked")
                    if D and n == SEL_AT:
                        ranks("sel_ready", sel, H, "sel_ranked")
                    if not A:
                        continue
                    m = n // 2
                    g, kc = m // 6, m % 6
                    if n >= 2:
                        pe.wait_ge(S["exp_done"], at(ka, 48, n - 1))
                    for a in range(2):
                        h = 4 * (g // 2) + 2 * (n % 2) + a
                        ins = t.matmul(PS[n % 2][:, a, 0:HALF], KS[:, h, kc * 128:(kc + 1) * 128],
                                       QS[:, h, (g % 2) * HALF:(g % 2 + 1) * HALF], start=True, stop=True)
                    ins.then_inc(S["s_ps"], 1)
                    if n % 2 and m >= 1:
                        weigh(m - 1)
                        if m % 6 == 2 and m >= 8:
                            turn_heads(m // 6 - 1)
                if A:
                    weigh(23)
                    turn_heads(3)
                if A:
                    pe.wait_ge(S["o_ready"], at(ka, 4, 4))
                    turn(U, PS[1])
                    pe.wait_ge(S["tt_ready"], at(ka, 4, 2))
                    project_rows(PS[0], Wo[:, :], S["wo_ps"])
                if D:
                    gate_logits(0, 10)
                if A:
                    pe.wait_ge(S["tokens_ready"], at(ka, 3, 2))
                    turn(TK, PS[1])
                    pe.wait_ge(S["tt_ready"], at(ka, 4, 3))
                    project(PS[0], W1[:, 0:C], S["h_ps"])
                    project(PS[1], W1[:, C:2 * C], S["h_ps"])
                if D:
                    gate_logits(10, 16)
                if A:
                    pe.wait_ge(S["h_ready"], at(ka, 2, 2))
                    for c in range(NCH):
                        for b in range(2):
                            ins = t.matmul(PS[0][:, c // 3, (c % 3) * 128:(c % 3) * 128 + 128],
                                           HT[b][:, c // 3, (c % 3) * 128:(c % 3) * 128 + 128], W2[:, b, :],
                                           start=(b == 0), stop=(b == 1))
                    ins.then_inc(S["ff_ps"], 1)
                if D:
                    the_list()
                    gate_logits(16, LG)
                    pe.wait_ge(S["lg_staged"], at(kd, LG, LG))
                if A:
                    pe.wait_ge(S["tokens_ready"], at(ka, 3, 3))
                    turn(U, PS[1])
                    pe.wait_ge(S["tt_ready"], at(ka, 4, 4))
                    project(PS[0], WG[:, NTAP:MAPS], S["sel_lg_ps"])
                if D:
                    pe.wait_ge(S["rows_known"], at(kd, 1, 1))
                if A:
                    pe.wait_ge(S["sel_lg_ready"], at(ka, 1, 1))

            rounds(pe, one)


def pick_phase(nc, B, io, scr, outer):
    ctx = ExitStack()
    with ctx:
        def sb(name, shape, dt=F32):
            return ctx.enter_context(nc.sbuf_tensor(name, shape, dt))

        sem = outer["sem"]
        K, topv, rows, PT = outer["K"], outer["topv"], outer["rows"], outer["PT"]
        L = [sb(f"L{u}", [128, ROWS]) for u in range(2)]
        ex = sb("ex", [128, ROWS], BF16)
        mval, pv8, pbase, eps5 = sb("mval", [128, TOPE]), sb("pv8", [128, TOPE]), sb("pbase", [128, 1]), sb("eps5", [128, 1])
        nmax, z, rz = sb("nmax", [128, 1]), sb("z", [128, 1]), sb("rz", [128, 1])
        mi = sb("mi", [128, TOPE], U32)
        ri = sb("ri", [128, TOPE], U32)
        rf = sb("rf", [128, TOPE])
        XG = sb("XG", [128, TOPE, C])
        XN = sb("XN", [128, TOPE, C])
        bs = sb("pbs", [128, TOPE, 6])
        bh = sb("pbh", [128, TOPE])
        mv = sb("pmv", [128, TOPE, 2])
        sd, rs = sb("psd", [128, TOPE]), sb("prs", [128, TOPE])
        pooled = sb("pooled", [128, C])
        ps = outer["psum"][0]
        own_sem = sem("pick_own")
        S = {n: sem("pick_" + n) for n in """l_in max_ready exp_done idx_ready rows_in kept var_ready sd_ready
            pooled_ready turned pair_done""".split()}
        at = lambda k, per, n: k * per + n
        PER = 60
        block = ctx.enter_context(nc.Block())

        @block.sync
        def _(sp):
            sp.sem_inc(S["pair_done"], 2)
            with sp.Fori(0, B // 4) as j:
              for u in range(2):
                i = j * 2 + u
                sp.wait_ge(S["pair_done"], at(i, 1, 1))
                sp.dma_start(L[u][:, :],
                             scr["logits"][bass.ds(i * 2, 2), :, :].rearrange("a e n -> (a e) n")).then_inc(S["l_in"], 16)
                sp.wait_ge(S["l_in"], at(i, 16, 16))
                hold(sp, outer["sp_held"])

        @block.gpsimd
        def _(pool):
            with pool.Fori(0, B // 4) as j:
              for u in range(2):
                i = j * 2 + u
                pool.wait_ge(S["idx_ready"], at(i, 1, 1))
                hold(pool, outer["pool_held"])
                for n in range(TOPE):
                    pool.indirect_dma_start(XG[:, n, :], None, scr["table"][:, :],
                                            bass.IndirectOffsetOnAxis(ap=ri[:, n:n + 1], axis=0)
                                            ).then_inc(S["rows_in"], 16)
                pool.wait_ge(S["rows_in"], at(i, 16 * TOPE, 16 * TOPE))
                hold(pool, outer["pool_held"])
                pool.dma_start(scr["picked"][bass.ds(i * 128, 128), :], XG[:, :, :].rearrange("p k c -> p (k c)")
                               ).then_inc(S["kept"], 16)
            pool.wait_ge(S["kept"], 16 * (B // 2))

        @block.scalar
        def _(act):
            with act.Fori(0, B // 4) as j:
              for u in range(2):
                i = j * 2 + u
                act.wait_ge(S["max_ready"], at(i, 1, 1))
                nc.scalar.activation(pv8[:, :], mval[:, :], ACT.Exp, bias=nmax[:, 0:1])
                nc.scalar.activation(ex[:, :], L[u][:, :], ACT.Exp, bias=nmax[:, 0:1],
                                     accum_out=z[:, 0:1]).then_inc(S["exp_done"], 1)
                act.wait_ge(S["var_ready"], at(i, 1, 1))
                nc.scalar.activation(sd[:, :], mv[:, :, 1], ACT.Sqrt, bias=eps5[:, 0:1]).then_inc(S["sd_ready"], 1)
                act.wait_ge(S["exp_done"], at(i, 1, 1))

        @block.vector
        def _(dve):
            v = nc.vector
            once = Own(dve, own_sem, 0, PER)
            once.step(v.memset(eps5[:, :], 1e-5))
            once.link(v.tensor_copy(pbase[:, :], K[:, C_S1:C_S1 + 1]))
            once.pad()
            with dve.Fori(0, B // 4) as j:
              for u in range(2):
                i = j * 2 + u
                own = Own(dve, own_sem, i, PER, before=PER)
                link, step = own.link, own.step
                Li = L[u][:, :]
                dve.wait_ge(S["l_in"], at(i, 16, 16))
                hold(dve, outer["dve_held"])
                link(v.max(mval[:, :], Li))
                v.tensor_scalar(nmax[:, :], mval[:, 0:1], -1.0, None, ALU.mult).then_inc(S["max_ready"], 1)
                link(v.max_index(mi[:, :], mval[:, :], Li))
                link(v.tensor_copy(rf[:, :], mi[:, :]))
                link(v.tensor_scalar(rf[:, :], rf[:, :], pbase[:, 0:1], None, ALU.add))
                step(v.tensor_scalar(pbase[:, :], pbase[:, :], 2.0 * ROWS, None, ALU.add))
                step(v.tensor_copy(rows[:, bass.ds(i * TOPE, TOPE)], rf[:, :]))
                v.tensor_copy(ri[:, :], rf[:, :]).then_inc(S["idx_ready"], 1)
                dve.wait_ge(S["exp_done"], at(i, 1, 1))
                link(v.reciprocal(rz[:, :], z[:, :]))
                link(v.tensor_scalar(pv8[:, :], pv8[:, :], rz[:, 0:1], None, ALU.mult))
                step(v.tensor_copy(topv[:, bass.ds(i * TOPE, TOPE)], pv8[:, :]))
                dve.wait_ge(S["rows_in"], at(i, 16 * TOPE, 16 * TOPE))
                for n in range(TOPE):
                    step(v.bn_stats(bs[:, n, :], XG[:, n, :]))
                own.wait()
                combine(v, own, mv, bs, bh)
                dve.sem_inc(S["var_ready"], 1)
                dve.wait_ge(S["sd_ready"], at(i, 1, 1))
                link(v.reciprocal(rs[:, :], sd[:, :]))
                link(v.tensor_tensor(rs[:, :], rs[:, :], pv8[:, :], ALU.mult))
                for n in range(TOPE):
                    step(v.tensor_scalar(XN[:, n, :], XG[:, n, :], mv[:, n, 0:1], rs[:, n:n + 1], ALU.subtract, ALU.mult))
                own.wait()
                v.tensor_reduce(pooled[:, :], XN[:, :, :].rearrange("p k c -> p c k"), AX.X, ALU.add
                                ).then_inc(S["pooled_ready"], 1)
                dve.wait_ge(S["turned"], at(i, 1, 1))
                v.tensor_copy(PT[:, bass.ds(i * 128, 128)], ps[:, 0:128]).then_inc(S["pair_done"], 1)
                own.pad()
                dve.wait_ge(S["kept"], at(i, 16, 16))

        @block.tensor
        def _(pe):
            with pe.Fori(0, B // 4) as j:
              for u in range(2):
                i = j * 2 + u
                pe.wait_ge(S["pooled_ready"], at(i, 1, 1))
                nc.tensor.transpose(ps[:, 0:128], pooled[:, :], K[:, C_ID:C_ID + 128]).then_inc(S["turned"], 1)


def expert_phase(nc, B, io, scr, outer):
    ctx = ExitStack()
    with ctx:
        def sb(name, shape, dt=F32):
            return ctx.enter_context(nc.sbuf_tensor(name, shape, dt))

        sem = outer["sem"]
        K, PT = outer["K"], outer["PT"]
        PTv = PT[:, :].rearrange("d (b e) -> d e b", e=E)
        W1S = [sb(f"W1S{i}", [C, 4, HID]) for i in range(2)]
        W1B = [sb(f"W1B{i}", [1, 4, HID]) for i in range(2)]
        W2S = [sb(f"W2S{i}", [128, 4, 4, C]) for i in range(2)]
        W2B = [sb(f"W2B{i}", [1, 4, C]) for i in range(2)]
        PTE = [sb(f"PTE{i}", [C, 4, 32]) for i in range(2)]
        HS = [sb(f"HS{i}", [128, HID]) for i in range(2)]
        HST = [sb(f"HST{i}", [128, 4, 128]) for i in range(2)]
        OS = [sb(f"OS{i}", [128, C]) for i in range(2)]
        psH = [outer["psum"][i] for i in range(2)]
        psT = [outer["psum"][2 + i] for i in range(2)]
        psO = [outer["psum2"][i][:, 0, :] for i in range(2)]
        w_in = [sem(f"w_in{i}") for i in range(2)]
        S = {n: sem("ex_" + n) for n in "zeroed picked h_ps h_ready hT_ps hT_ready o_ps o_ready stored0 stored1".split()}
        at = lambda k, per, n: k * per + n
        block = ctx.enter_context(nc.Block())
        NG = E // 4

        @block.sync
        def _(sp):
            sp.sem_inc(S["o_ps"], 2)
            with sp.Fori(0, NG // 2) as i:
                for u in range(2):
                    sp.wait_ge(S["o_ps"], at(i, 2, u + 1))
                    e = i * 8 + 4 * u
                    sp.dma_start(W1S[u][:, :, :], io["weight1"][bass.ds(e, 4), 0:C, :].rearrange("e d n -> d e n")
                                 ).then_inc(w_in[u], 16)
                    sp.dma_start(W1B[u][:, :, :], io["weight1"][bass.ds(e, 4), C:C + 1, :].rearrange("e d n -> d e n")
                                 ).then_inc(w_in[u], 16)
                    for c in range(4):
                        sp.dma_start(W2S[u][:, :, c, :], io["weight2"][bass.ds(e, 4), c * 128:(c + 1) * 128, :].rearrange(
                            "e p n -> p e n")).then_inc(w_in[u], 16)
                    sp.dma_start(W2B[u][:, :, :], io["weight2"][bass.ds(e, 4), HID:HID + 1, :].rearrange("e d n -> d e n")
                                 ).then_inc(w_in[u], 16)

        @block.gpsimd
        def _(pool):
            with pool.Fori(0, NG // 2) as i:
                for u in range(2):
                    pool.wait_ge(S["o_ready"], at(i, 2, u + 1))
                    hold(pool, outer["pool_held"])
                    for j in range(4):
                        pool.dma_start(scr["expert_out"][:, bass.ds(i * 8 + 4 * u + j, 1), :].rearrange("b a c -> b (a c)"),
                                       OS[u][32 * j:32 * j + B, :]).then_inc(S[f"stored{u}"], 16)
            for u in range(2):
                pool.wait_ge(S[f"stored{u}"], NG // 2 * 64)

        @block.vector
        def _(dve):
            v = nc.vector
            for u in range(2):
                v.memset(PTE[u][:, :, :], 0.0).then_inc(S["zeroed"], 1)
            dve.wait_ge(S["zeroed"], 2)
            with dve.Fori(0, NG // 2) as i:
                for u in range(2):
                    dve.wait_ge(S["o_ps"], at(i, 2, u + 1))
                    v.tensor_copy(PTE[u][:, :, 0:B], PTv[:, bass.ds(i * 8 + 4 * u, 4), :]).then_inc(S["picked"], 1)
                for u in range(2):
                    dve.wait_ge(S["hT_ps"], at(i, 2, u + 1))
                    v.tensor_copy(HST[u][:, :, :], psT[u][:, :].rearrange("p (c n) -> p c n", c=4)).then_inc(S["hT_ready"], 1)
                    dve.wait_ge(S["o_ps"], at(i, 2, u + 3))
                    v.tensor_copy(OS[u][:, :], psO[u][:, 0:C]).then_inc(S["o_ready"], 1)
                for u in range(2):
                    dve.wait_ge(S[f"stored{u}"], at(i, 64, 64))

        @block.scalar
        def _(act):
            with act.Fori(0, NG // 2) as i:
                for u in range(2):
                    act.wait_ge(S["h_ps"], at(i, 2, u + 1))
                    nc.scalar.activation(HS[u][:, :], psH[u][:, :], ACT.Gelu).then_inc(S["h_ready"], 1)

        @block.tensor
        def _(pe):
            t = nc.tensor
            ones = K[0:1, C_ONE:C_ONE + 32]
            with pe.Fori(0, NG // 2) as i:
                for u in range(2):
                    pe.wait_ge(w_in[u], at(i, 7 * 16, 7 * 16))
                    pe.wait_ge(S["picked"], at(i, 2, u + 1))
                    for j in range(4):
                        t.matmul(psH[u][32 * j:32 * j + 32, :], PTE[u][:, j, :], W1S[u][:, j, :], start=True, stop=False)
                    for j in range(4):
                        ins = t.matmul(psH[u][32 * j:32 * j + 32, :], ones, W1B[u][:, j, :], start=False, stop=True)
                    ins.then_inc(S["h_ps"], 1)
                for u in range(2):
                    pe.wait_ge(S["h_ready"], at(i, 2, u + 1))
                    for c in range(4):
                        ins = t.transpose(psT[u][:, c * 128:(c + 1) * 128], HS[u][:, c * 128:(c + 1) * 128],
                                          K[:, C_ID:C_ID + 128])
                    ins.then_inc(S["hT_ps"], 1)
                    pe.wait_ge(S["hT_ready"], at(i, 2, u + 1))
                    for c in range(4):
                        for j in range(4):
                            t.matmul(psO[u][32 * j:32 * j + 32, 0:C], HST[u][:, c, 32 * j:32 * j + 32], W2S[u][:, j, c, :],
                                     start=(c == 0), stop=False)
                    for j in range(4):
                        ins = t.matmul(psO[u][32 * j:32 * j + 32, 0:C], ones, W2B[u][:, j, :], start=False, stop=True)
                    ins.then_inc(S["o_ps"], 1)
                pe.wait_ge(S["o_ready"], at(i, 2, 2))


def scatter_phase(nc, B, io, scr, outer):
    ctx = ExitStack()
    with ctx:
        def sb(name, shape, dt=F32):
            return ctx.enter_context(nc.sbuf_tensor(name, shape, dt))

        sem = outer["sem"]
        K, topv, rows, lists = outer["K"], outer["topv"], outer["rows"], outer["lists"]
        table = scr["table"]
        OE = sb("sOE", [128, C])
        XG = sb("sXG", [128, TOPE, C])
        WK = sb("WK", [128, TOPE, C])
        DG = sb("DG", [128, TOPE, 128])
        IR = sb("IR", [128, TOPE, 128])
        EQ = sb("EQ", [128, TOPE, TOPE, 128])
        EL = sb("EL", [128, TOPE, 128])
        rk, tv, dup = sb("rk", [128, TOPE]), sb("tv", [128, TOPE]), sb("dup", [128, TOPE])
        ri = sb("sri", [128, TOPE], U32)
        T6 = [sb(f"T6{s}", [128, NCH, C]) for s in range(2)]
        li = sb("li", [128, 2 * NCH], U32)
        own_sem = sem("sc_own")
        S = {n: sem("sc_" + n) for n in """loaded diag_ready spread_ps eq_ready sums_ps rows_ready scattered
            tokens_in tokens_out tokens_done""".split()}
        at = lambda k, per, n: k * per + n
        PER = 60
        psA = outer["psum2"][0]
        psB = outer["psum2"][1]
        psC = outer["psum"][0]
        block = ctx.enter_context(nc.Block())

        @block.sync
        def _(sp):
            with sp.Fori(0, B // 2) as i:
                sp.dma_start(OE[:, :], scr["expert_out"][bass.ds(i * 2, 2), :, :].rearrange("a e c -> (a e) c")
                             ).then_inc(S["loaded"], 16)
                sp.dma_start(XG[:, :, :].rearrange("p k c -> p (k c)"), scr["picked"][bass.ds(i * 128, 128), :]
                             ).then_inc(S["loaded"], 16)
                sp.wait_ge(S["scattered"], at(i, 16 * TOPE, 16 * TOPE))
                for s in range(2):
                    sp.dma_start(T6[s][:, :, :], table[bass.ds(i * 2 * ROWS + s * ROWS + NPIX, KTOK), :].rearrange(
                        "(t p) c -> p t c", p=128)).then_inc(S["tokens_in"], 16)

        @block.gpsimd
        def _(pool):
            pool.sem_inc(S["tokens_done"], 1)
            with pool.Fori(0, B // 2) as i:
                pool.wait_ge(S["rows_ready"], at(i, 1, 1))
                hold(pool, outer["pool_held"])
                for n in range(TOPE):
                    pool.indirect_dma_start(table[:, :], bass.IndirectOffsetOnAxis(ap=ri[:, n:n + 1], axis=0),
                                            XG[:, n, :], None, bounds_check=B * ROWS - 1, oob_is_err=False
                                            ).then_inc(S["scattered"], 16)
                pool.wait_ge(S["tokens_in"], at(i, 32, 32))
                hold(pool, outer["pool_held"])
                for n in range(2 * NCH):
                    pool.indirect_dma_start(table[:, :], bass.IndirectOffsetOnAxis(ap=li[:, n:n + 1], axis=0),
                                            T6[n // NCH][:, n % NCH, :], None).then_inc(S["tokens_out"], 16)
                pool.wait_ge(S["tokens_out"], at(i, 2 * NCH * 16, 2 * NCH * 16))
                pool.sem_inc(S["tokens_done"], 1)
            pool.wait_ge(S["scattered"], B // 2 * 16 * TOPE)
            pool.wait_ge(S["tokens_out"], B // 2 * 2 * NCH * 16)

        @block.vector
        def _(dve):
            v = nc.vector
            with dve.Fori(0, B // 2) as i:
                own = Own(dve, own_sem, i, PER)
                link, step = own.link, own.step
                step(v.tensor_copy(rk[:, :], rows[:, bass.ds(i * TOPE, TOPE)]))
                link(v.tensor_copy(tv[:, :], topv[:, bass.ds(i * TOPE, TOPE)]))
                v.tensor_tensor(DG[:, :, :], bc(K[:, C_ID:C_ID + 128], [128, TOPE, 128], 1), bc(rk[:, :], [128, TOPE, 128], 2),
                                ALU.mult).then_inc(S["diag_ready"], 1)
                dve.wait_ge(S["loaded"], at(i, 32, 32))
                for n in range(TOPE):
                    step(v.tensor_scalar(WK[:, n, :], OE[:, :], tv[:, n:n + 1], None, ALU.mult))
                dve.wait_ge(S["spread_ps"], at(i, 1, 1))
                link(v.tensor_copy(IR[:, :, :].rearrange("p (a k) n -> p a (k n)", a=2), psA[:, :, :]))
                for n in range(TOPE):
                    step(v.tensor_scalar(EQ[:, n, :, :], IR[:, :, :], rk[:, n:n + 1], None, ALU.is_equal))
                own.wait()
                for n in range(TOPE):
                    step(v.tensor_tensor(EL[:, n, :], EQ[:, n, n, :], K[:, C_LT:C_LT + 128], ALU.mult))
                own.wait()
                dve.sem_inc(S["eq_ready"], 1)
                dve.wait_ge(S["sums_ps"], at(i, 1, 1))
                link(v.tensor_tensor(XG[:, :, :].rearrange("p (a k) c -> p a (k c)", a=2),
                                     XG[:, :, :].rearrange("p (a k) c -> p a (k c)", a=2), psB[:, :, :], ALU.add))
                link(v.tensor_scalar(dup[:, :], psC[:, 0:TOPE], 0.5, FAR, ALU.is_ge, ALU.mult))
                link(v.tensor_tensor(dup[:, :], dup[:, :], rk[:, :], ALU.add))
                dve.wait_ge(S["tokens_done"], at(i, 1, 1))
                step(v.tensor_copy(li[:, :], lists[:, bass.ds(i * 2 * NCH, 2 * NCH)]))
                link(v.tensor_copy(ri[:, :], dup[:, :]))
                dve.sem_inc(S["rows_ready"], 1)
                own.pad()

        @block.tensor
        def _(pe):
            t = nc.tensor
            with pe.Fori(0, B // 2) as i:
                pe.wait_ge(S["diag_ready"], at(i, 1, 1))
                for a in range(2):
                    ins = t.matmul(psA[:, a, :], K[:, C_ONE:C_ONE + 128],
                                   DG[:, 4 * a:4 * a + 4, :].rearrange("p k n -> p (k n)"), start=True, stop=True)
                ins.then_inc(S["spread_ps"], 1)
                pe.wait_ge(S["eq_ready"], at(i, 1, 1))
                for m in range(TOPE):
                    for n in range(TOPE):
                        t.matmul(psB[:, m // 4, (m % 4) * 128:(m % 4) * 128 + 128], EQ[:, n, m, :], WK[:, n, :],
                                 start=(n == 0), stop=(n == TOPE - 1))
                for m in range(TOPE):
                    for n in range(m):
                        t.matmul(psC[:, m:m + 1], EQ[:, n, m, :], K[:, C_ONE:C_ONE + 1], start=(n == 0), stop=False)
                    ins = t.matmul(psC[:, m:m + 1], EL[:, m, :], K[:, C_ONE:C_ONE + 1], start=(m == 0), stop=True)
                ins.then_inc(S["sums_ps"], 1)


def output_phase(nc, B, io, scr, outer):
    ctx = ExitStack()
    with ctx:
        def sb(name, shape, dt=F32):
            return ctx.enter_context(nc.sbuf_tensor(name, shape, dt))

        sem = outer["sem"]
        K = outer["K"]
        NT, PX = 11, 10
        RING = 4
        FT = [sb(f"FT{i}", [H, PX, C]) for i in range(RING)]
        OT = [sb(f"OT{i}", [C, H, PX]) for i in range(RING)]
        parts = [(0, 4), (4, 4), (8, 2)]
        ps = [[outer["psum2"][i][:, 0, :], outer["psum2"][i][:, 1, :], outer["psum"][i][:, :]] for i in range(2)]
        f_in = [sem(f"f_in{i}") for i in range(RING)]
        f_out = [sem(f"f_out{i}") for i in range(RING)]
        S = {n: sem("out_" + n) for n in "turned act_copied dve_copied".split()}
        at = lambda k, per, n: k * per + n
        block = ctx.enter_context(nc.Block())
        TWO = 2 * NT
        USES = [len(range(i, TWO, RING)) for i in range(RING)]

        def table_rows(k, s, tile):
            return scr["table"][bass.ds(k * 2 * ROWS + s * ROWS + tile * H * PX, H * PX), :].rearrange(
                "(p a) c -> p a c", a=PX)

        def copies(eng, k, fn, name, mine):
            for n in range(TWO):
                eng.wait_ge(S["turned"], at(k, TWO, TWO + n + 1))
                if n >= RING:
                    eng.wait_ge(f_out[n % RING], at(k, USES[n % RING] * 16, 16 * (n // RING)))
                for part in mine(n):
                    a, m = parts[part]
                    ins = fn(OT[n % RING][:, :, a:a + m].rearrange("c p a -> c a p"),
                             ps[n % 2][part][:, 0:m * H].rearrange("c (a p) -> c a p", a=m))
                ins.then_inc(S[name], 1)
            for i in range(RING):
                eng.wait_ge(f_out[i], at(k, USES[i] * 16, USES[i] * 16))

        @block.sync
        def _(sp):
            with sp.Fori(0, B // 2) as k:
                for n in range(TWO):
                    s, tile = n // NT, n % NT
                    before = n - RING if n >= RING else RING * (USES[n] - 1) + n - TWO
                    sp.wait_ge(S["turned"], at(k, TWO, TWO + before + 1))
                    sp.dma_start(FT[n % RING][:, :, :], table_rows(k, s, tile)).then_inc(f_in[n % RING], 16)

        @block.gpsimd
        def _(pool):
            with pool.Fori(0, B // 2) as k:
                for n in range(TWO):
                    s, tile = n // NT, n % NT
                    pool.wait_ge(S["act_copied"], at(k, TWO, TWO + n + 1))
                    pool.wait_ge(S["dve_copied"], at(k, TWO, TWO + n + 1))
                    hold(pool, outer["pool_held"])
                    pool.dma_start(io["out"][bass.ds(k * 2 + s, 1), :, tile * H * PX:(tile + 1) * H * PX].rearrange(
                        "b c n -> (b c) n"), OT[n % RING][:, :, :].rearrange("c p a -> c (p a)")).then_inc(f_out[n % RING], 16)
            for i in range(RING):
                pool.wait_ge(f_out[i], B // 2 * USES[i] * 16)

        @block.scalar
        def _(act):
            act.sem_inc(S["act_copied"], TWO)
            with act.Fori(0, B // 2) as k:
                copies(act, k, lambda o, i: nc.scalar.activation(o, i, ACT.Copy), "act_copied",
                       lambda n: (0,) if n % 2 else (0, 2))

        @block.vector
        def _(dve):
            dve.sem_inc(S["dve_copied"], TWO)
            with dve.Fori(0, B // 2) as k:
                copies(dve, k, lambda o, i: nc.vector.tensor_copy(o, i), "dve_copied",
                       lambda n: (1, 2) if n % 2 else (1,))

        @block.tensor
        def _(pe):
            pe.sem_inc(S["turned"], TWO)
            with pe.Fori(0, B // 2) as k:
                for n in range(TWO):
                    pe.wait_ge(f_in[n % RING], at(k, USES[n % RING] * 16, 16 * (n // RING + 1)))
                    pe.wait_ge(S["act_copied"], at(k, TWO, TWO + n - 1))
                    pe.wait_ge(S["dve_copied"], at(k, TWO, TWO + n - 1))
                    for part, (a, m) in enumerate(parts):
                        for j in range(m):
                            ins = nc.tensor.transpose(ps[n % 2][part][:, j * H:(j + 1) * H], FT[n % RING][:, a + j, :],
                                                      K[0:H, C_ID:C_ID + H])
                    ins.then_inc(S["turned"], 1)


def build(nc, B, io, scr):
    with ExitStack() as ctx:
        outer = {
            "sem": lambda name: ctx.enter_context(nc.semaphore(name)),
            "K": ctx.enter_context(nc.sbuf_tensor("K", [128, NCONST], F32)),
            "lists": ctx.enter_context(nc.sbuf_tensor("lists", [128, B * NCH], U32)),
            "topv": ctx.enter_context(nc.sbuf_tensor("topv", [128, B // 2 * TOPE], F32)),
            "rows": ctx.enter_context(nc.sbuf_tensor("rows", [128, B // 2 * TOPE], F32)),
            "psum2": [ctx.enter_context(nc.psum_tensor(f"pair{i}", [128, 2, 512], F32)) for i in range(2)],
            "psum": [ctx.enter_context(nc.psum_tensor(f"bank{i}", [128, 512], F32)) for i in range(4)],
        }
        for name in ("pool_held", "pe_held", "sp_held", "dve_held"):
            outer[name] = outer["sem"](name)
        nc.disable_value_cache = True
        token_phase(nc, B, io, scr, outer)
        nc.disable_value_cache = False
        outer["PT"] = ctx.enter_context(nc.sbuf_tensor("PT", [C, B * E], F32))
        pick_phase(nc, B, io, scr, outer)
        expert_phase(nc, B, io, scr, outer)
        scatter_phase(nc, B, io, scr, outer)
        output_phase(nc, B, io, scr, outer)


def kernel(**inputs):
    import concourse.bacc as _bacc
    from concourse.bass_utils import run_bass_kernel_spmd as _run

    def g(name):
        return np.asarray(inputs[name])

    x = g("x")
    B = x.shape[0]
    b_qkv, b1 = g("L0_conv_b_qkv"), g("L0_conv_b1")
    arrays = {
        "x": x.reshape(B, C, NPIX), "conv_w": g("L0_conv_conv_w").reshape(C, NTAP), "gateT": g("L0_ffn_gate_w").T,
        "wqkvT": g("L0_conv_w_qkv").T, "woT": g("L0_conv_w_o").T, "w1T": g("L0_conv_w1").T, "w2T": g("L0_conv_w2").T,
        "bq": b_qkv[:C], "bk": b_qkv[C:2 * C], "bv": b_qkv[2 * C:], "b_o": g("L0_conv_b_o"),
        "ln1_g": g("L0_conv_ln1_g"), "ln1_b": g("L0_conv_ln1_b"), "b1a": b1[:C], "b1b": b1[C:], "b2": g("L0_conv_b2"),
        "ln2_g": g("L0_conv_ln2_g"), "ln2_b": g("L0_conv_ln2_b"), "gate_b": g("L0_ffn_gate_b"),
        "conv_b": g("L0_conv_conv_b"), "bn_g": g("L0_conv_bn_g"), "bn_b": g("L0_conv_bn_b"),
        "bn_m": g("L0_conv_bn_m"), "bn_v": g("L0_conv_bn_v"), "weight1": g("L0_ffn_weight1"),
        "weight2": g("L0_ffn_weight2"), "const": constants(), "pos": positions(),
    }
    arrays = {n: np.ascontiguousarray(a) for n, a in arrays.items()}
    nc = _bacc.Bacc("TRN2", target_bir_lowering=False, num_devices=1)
    io = {n: nc.dram_tensor("in_" + n, a.shape, F32, kind="ExternalInput").ap() for n, a in arrays.items()}
    io["out"] = nc.dram_tensor("out", (B, C, NPIX), F32, kind="ExternalOutput").ap()
    scr = {
        "parts": nc.dram_tensor("parts", (2, C, 3, KTOK), BF16, kind="Internal").ap(),
        "current": nc.dram_tensor("current", (NPIX, C), F32, kind="Internal").ap(),
        "table": nc.dram_tensor("table", (B * ROWS, C), F32, kind="Internal").ap(),
        "logits": nc.dram_tensor("logits", (B, E, ROWS), F32, kind="Internal").ap(),
        "picked": nc.dram_tensor("picked", (B // 2 * 128, TOPE * C), F32, kind="Internal").ap(),
        "expert_out": nc.dram_tensor("expert_out", (B, E, C), F32, kind="Internal").ap(),
    }
    build(nc, B, io, scr)
    r = _run(nc, [{"in_" + n: a for n, a in arrays.items()}], core_ids=[0])
    return r.results[0]["out"].reshape(B, C, H, H)
```
